# Optimizing a Trainium2 kernel written in Bass

```python
import numpy as np
import jax
import jax.numpy as jnp

def _softmax(x, axis=-1):
    return jax.nn.softmax(x, axis=axis)

def _gelu(x):
    return jax.nn.gelu(x, approximate=True)

def _silu(x):
    return jax.nn.silu(x)

def _sigmoid(x):
    return jax.nn.sigmoid(x)

def _layernorm(x, axis=-1, eps=1e-05):
    m = jnp.mean(x, axis=axis, keepdims=True)
    v = jnp.var(x, axis=axis, keepdims=True)
    return (x - m) / jnp.sqrt(v + eps)

def _scatter_add(tgt, idx, src, axis=0):
    return tgt.at[idx].add(src)

def _segment_sum(src, seg, n):
    return jax.ops.segment_sum(src, seg, n)
kernel_name = 'mk_cond_seq_d2_seqx_r4_29a394'

def setup_inputs(seed: int=0):
    np.random.seed(seed)
    _w = jnp.asarray

    def _rec_inputs():
        import jax
        import jax.numpy as jnp
        _rk = jax.random.key(seed)
        x = 7.22e-05 + 1 * jax.random.normal(jax.random.fold_in(_rk, 1), (16, 256, 256), jnp.float32)
        _lenS = 256 - jax.random.randint(jax.random.fold_in(_rk, 7), (16,), 0, max(1, 256 // 4) + 1, jnp.int32)
        _lenS2 = 256 - jax.random.randint(jax.random.fold_in(_rk, 8), (16,), 0, max(1, 256 // 4) + 1, jnp.int32)
        cond_2048 = 0.00782532 + 1.00527 * jax.random.normal(jax.random.fold_in(_rk, 11), (16, 512), jnp.float32)
        _validS = jnp.arange(256)[None, :] < _lenS[:, None]
        _validS2 = jnp.arange(256)[None, :] < _lenS2[:, None]
        _causal = jnp.tril(jnp.ones((256, 256), dtype=bool))
        mask_BxSx1_fk1 = jnp.where(jnp.ones((16, 256, 1), dtype=bool), 1.0, 0.0).astype(jnp.float32)
        mask_BxS_ik0 = jnp.where(jnp.broadcast_to(_validS[:, :], (16, 256)), 0, 1).astype(jnp.int32)
        return (x, cond_2048, mask_BxSx1_fk1, mask_BxS_ik0)
    x, cond_2048, mask_BxSx1_fk1, mask_BxS_ik0 = _rec_inputs()

    def _L0_cond_setup():
        import jax, jax.numpy as jnp
        import numpy as np
        B, T, D, H, TE = (4, 512, 256, 8, 512)
        EPS = 1e-05

        def _ln(x, w, b):
            m = jnp.mean(x, axis=-1, keepdims=True)
            v = jnp.mean((x - m) ** 2, axis=-1, keepdims=True)
            return (x - m) * jax.lax.rsqrt(v + EPS) * w + b
        key = jax.random.key(seed)
        ks = jax.random.split(key, 16)
        s = 0.02
        inp = {'x': jax.random.normal(ks[0], (B, T, D), jnp.float32), 'emb': jax.random.normal(ks[1], (B, TE), jnp.float32), 'src_mask': (jax.random.uniform(ks[2], (B, T, 1)) > 0.2).astype(jnp.float32), 'num_head': H, 'ln_w': jnp.ones((D,), jnp.float32), 'ln_b': jnp.zeros((D,), jnp.float32), 'Wq': jax.random.normal(ks[3], (D, D), jnp.float32) * s, 'bq': jnp.zeros((D,), jnp.float32), 'Wk': jax.random.normal(ks[4], (D, D), jnp.float32) * s, 'bk': jnp.zeros((D,), jnp.float32), 'Wv': jax.random.normal(ks[5], (D, D), jnp.float32) * s, 'bv': jnp.zeros((D,), jnp.float32), 'W_emb': jax.random.normal(ks[6], (TE, 2 * D), jnp.float32) * s, 'b_emb': jnp.zeros((2 * D,), jnp.float32), 'ln2_w': jnp.ones((D,), jnp.float32), 'ln2_b': jnp.zeros((D,), jnp.float32), 'W_out': jax.random.normal(ks[7], (D, D), jnp.float32) * s, 'b_out': jnp.zeros((D,), jnp.float32)}
        return inp
    _L0_cond_all = _L0_cond_setup()
    _L0_cond_in = {k: v for k, v in _L0_cond_all.items() if k in ('ln_w', 'ln_b', 'Wq', 'bq', 'Wk', 'bk', 'Wv', 'bv', 'W_emb', 'b_emb', 'ln2_w', 'ln2_b', 'W_out', 'b_out')}
    del _L0_cond_all

    def _L1_cond_setup():
        import jax, jax.numpy as jnp
        import numpy as np
        H = 16
        LN_EPS = 1e-05

        def _layernorm(x, scale, bias):
            mu = jnp.mean(x, axis=-1, keepdims=True)
            var = jnp.var(x, axis=-1, keepdims=True)
            return (x - mu) * jax.lax.rsqrt(var + LN_EPS) * scale + bias
        key = jax.random.key(seed)
        ks = jax.random.split(key, 8)
        B, T, D, E = (4, 1024, 256, 512)
        s = 0.02
        return {'x': jax.random.normal(ks[0], (B, T, D), jnp.float32), 'emb': jax.random.normal(ks[1], (B, E), jnp.float32), 'src_mask': jax.random.randint(ks[2], (B, T), 0, 2).astype(jnp.int32), 'norm_scale': jnp.ones((D,), jnp.float32), 'norm_bias': jnp.zeros((D,), jnp.float32), 'Wq': jax.random.normal(ks[3], (D, D), jnp.float32) * s, 'bq': jnp.zeros((D,), jnp.float32), 'Wk': jax.random.normal(ks[4], (D, D), jnp.float32) * s, 'bk': jnp.zeros((D,), jnp.float32), 'Wv': jax.random.normal(ks[5], (D, D), jnp.float32) * s, 'bv': jnp.zeros((D,), jnp.float32), 'film_emb_W': jax.random.normal(ks[6], (E, 2 * D), jnp.float32) * s, 'film_emb_b': jnp.zeros((2 * D,), jnp.float32), 'film_norm_scale': jnp.ones((D,), jnp.float32), 'film_norm_bias': jnp.zeros((D,), jnp.float32), 'film_out_W': jax.random.normal(ks[7], (D, D), jnp.float32) * s, 'film_out_b': jnp.zeros((D,), jnp.float32)}
    _L1_cond_all = _L1_cond_setup()
    _L1_cond_in = {k: v for k, v in _L1_cond_all.items() if k in ('norm_scale', 'norm_bias', 'Wq', 'bq', 'Wk', 'bk', 'Wv', 'bv', 'film_emb_W', 'film_emb_b', 'film_norm_scale', 'film_norm_bias', 'film_out_W', 'film_out_b')}
    del _L1_cond_all
    return {'x': x, 'cond_2048': cond_2048, 'mask_BxSx1_fk1': mask_BxSx1_fk1, 'mask_BxS_ik0': mask_BxS_ik0, 'L0_cond_ln_w': _L0_cond_in['ln_w'], 'L0_cond_ln_b': _L0_cond_in['ln_b'], 'L0_cond_Wq': _L0_cond_in['Wq'], 'L0_cond_bq': _L0_cond_in['bq'], 'L0_cond_Wk': _L0_cond_in['Wk'], 'L0_cond_bk': _L0_cond_in['bk'], 'L0_cond_Wv': _L0_cond_in['Wv'], 'L0_cond_bv': _L0_cond_in['bv'], 'L0_cond_W_emb': _L0_cond_in['W_emb'], 'L0_cond_b_emb': _L0_cond_in['b_emb'], 'L0_cond_ln2_w': _L0_cond_in['ln2_w'], 'L0_cond_ln2_b': _L0_cond_in['ln2_b'], 'L0_cond_W_out': _L0_cond_in['W_out'], 'L0_cond_b_out': _L0_cond_in['b_out'], 'L1_cond_norm_scale': _L1_cond_in['norm_scale'], 'L1_cond_norm_bias': _L1_cond_in['norm_bias'], 'L1_cond_Wq': _L1_cond_in['Wq'], 'L1_cond_bq': _L1_cond_in['bq'], 'L1_cond_Wk': _L1_cond_in['Wk'], 'L1_cond_bk': _L1_cond_in['bk'], 'L1_cond_Wv': _L1_cond_in['Wv'], 'L1_cond_bv': _L1_cond_in['bv'], 'L1_cond_film_emb_W': _L1_cond_in['film_emb_W'], 'L1_cond_film_emb_b': _L1_cond_in['film_emb_b'], 'L1_cond_film_norm_scale': _L1_cond_in['film_norm_scale'], 'L1_cond_film_norm_bias': _L1_cond_in['film_norm_bias'], 'L1_cond_film_out_W': _L1_cond_in['film_out_W'], 'L1_cond_film_out_b': _L1_cond_in['film_out_b']}

def reference(x, cond_2048, mask_BxSx1_fk1, mask_BxS_ik0, L0_cond_ln_w, L0_cond_ln_b, L0_cond_Wq, L0_cond_bq, L0_cond_Wk, L0_cond_bk, L0_cond_Wv, L0_cond_bv, L0_cond_W_emb, L0_cond_b_emb, L0_cond_ln2_w, L0_cond_ln2_b, L0_cond_W_out, L0_cond_b_out, L1_cond_norm_scale, L1_cond_norm_bias, L1_cond_Wq, L1_cond_bq, L1_cond_Wk, L1_cond_bk, L1_cond_Wv, L1_cond_bv, L1_cond_film_emb_W, L1_cond_film_emb_b, L1_cond_film_norm_scale, L1_cond_film_norm_bias, L1_cond_film_out_W, L1_cond_film_out_b):
    import jax
    import jax.numpy as jnp

    def _L0_cond_ref(x, emb, src_mask, num_head, ln_w, ln_b, Wq, bq, Wk, bk, Wv, bv, W_emb, b_emb, ln2_w, ln2_b, W_out, b_out):
        import jax, jax.numpy as jnp
        import numpy as np
        B, T, D, H, TE = (4, 512, 256, 8, 512)
        EPS = 1e-05

        def _ln(x, w, b):
            m = jnp.mean(x, axis=-1, keepdims=True)
            v = jnp.mean((x - m) ** 2, axis=-1, keepdims=True)
            return (x - m) * jax.lax.rsqrt(v + EPS) * w + b
        b, t, d = x.shape
        h = num_head
        dh = d // h
        xn = _ln(x, ln_w, ln_b)
        q = xn @ Wq + bq
        k = xn @ Wk + bk + (1.0 - src_mask) * -1000000.0
        q = jax.nn.softmax(q.reshape(b, t, h, dh), axis=-1)
        k = jax.nn.softmax(k.reshape(b, t, h, dh), axis=1)
        v = ((xn @ Wv + bv) * src_mask).reshape(b, t, h, dh)
        att = jnp.einsum('bnhd,bnhl->bhdl', k, v)
        y = jnp.einsum('bnhd,bhdl->bnhl', q, att).reshape(b, t, d)
        emb_out = (jax.nn.silu(emb) @ W_emb + b_emb)[:, None, :]
        scale, shift = jnp.split(emb_out, 2, axis=2)
        hh = _ln(y, ln2_w, ln2_b) * (1.0 + scale) + shift
        hh = jax.nn.silu(hh) @ W_out + b_out
        return x + hh

    def _L1_cond_ref(x, emb, src_mask, norm_scale, norm_bias, Wq, bq, Wk, bk, Wv, bv, film_emb_W, film_emb_b, film_norm_scale, film_norm_bias, film_out_W, film_out_b):
        import jax, jax.numpy as jnp
        import numpy as np
        H = 16
        LN_EPS = 1e-05

        def _layernorm(x, scale, bias):
            mu = jnp.mean(x, axis=-1, keepdims=True)
            var = jnp.var(x, axis=-1, keepdims=True)
            return (x - mu) * jax.lax.rsqrt(var + LN_EPS) * scale + bias
        B, T, D = x.shape
        dh = D // H
        xn = _layernorm(x, norm_scale, norm_bias)
        q = xn @ Wq + bq
        k = xn @ Wk + bk
        v = xn @ Wv + bv
        mask = (src_mask == 1)[:, :, None]
        k = jnp.where(mask, -jnp.inf, k)
        v = jnp.where(mask, 0.0, v)
        q = q.reshape(B, T, H, dh).transpose(0, 2, 1, 3)
        k = k.reshape(B, T, H, dh).transpose(0, 2, 1, 3)
        v = v.reshape(B, T, H, dh).transpose(0, 2, 1, 3)
        q = jax.nn.softmax(q, axis=-1)
        k = jax.nn.softmax(k, axis=2)
        attn = jnp.einsum('bhse,bhsd->bhed', k, v)
        y = jnp.einsum('bhtd,bhed->bhte', q, attn)
        y = y.transpose(0, 2, 1, 3).reshape(B, T, D)
        emb_out = jax.nn.silu(emb) @ film_emb_W + film_emb_b
        scale, shift = jnp.split(emb_out, 2, axis=-1)
        h = _layernorm(y, film_norm_scale, film_norm_bias) * (1.0 + scale[:, None, :]) + shift[:, None, :]
        h = jax.nn.silu(h) @ film_out_W + film_out_b
        return x + h
    x = _L0_cond_ref(x, cond_2048, mask_BxSx1_fk1, 8, L0_cond_ln_w, L0_cond_ln_b, L0_cond_Wq, L0_cond_bq, L0_cond_Wk, L0_cond_bk, L0_cond_Wv, L0_cond_bv, L0_cond_W_emb, L0_cond_b_emb, L0_cond_ln2_w, L0_cond_ln2_b, L0_cond_W_out, L0_cond_b_out)
    x = _L1_cond_ref(x, cond_2048, mask_BxS_ik0, L1_cond_norm_scale, L1_cond_norm_bias, L1_cond_Wq, L1_cond_bq, L1_cond_Wk, L1_cond_bk, L1_cond_Wv, L1_cond_bv, L1_cond_film_emb_W, L1_cond_film_emb_b, L1_cond_film_norm_scale, L1_cond_film_norm_bias, L1_cond_film_out_W, L1_cond_film_out_b)
    return x

_drawn_inputs = setup_inputs


def setup_inputs(seed=0):
    import zlib

    import numpy as np

    out = dict(_drawn_inputs(seed))
    spreads = {'L0_cond_ln_w': (1.0, 0.6),
     'L0_cond_ln_b': (0.0, 0.1),
     'L0_cond_bq': (0.0, 0.8),
     'L0_cond_bk': (0.0, 2.0),
     'L0_cond_bv': (0.0, 0.1),
     'L0_cond_b_emb': (0.0, 0.1),
     'L0_cond_ln2_w': (1.0, 0.2),
     'L0_cond_ln2_b': (0.0, 0.463),
     'L0_cond_b_out': (0.0, 0.1),
     'L1_cond_norm_scale': (1.0, 0.6),
     'L1_cond_norm_bias': (0.0, 0.3),
     'L1_cond_bq': (0.0, 0.607),
     'L1_cond_bk': (0.0, 2.0),
     'L1_cond_bv': (0.0, 0.1),
     'L1_cond_film_emb_b': (0.0, 0.273),
     'L1_cond_film_norm_scale': (1.0, 0.2),
     'L1_cond_film_norm_bias': (0.0, 0.358),
     'L1_cond_film_out_b': (0.0, 0.1)}
    factors = {'L0_cond_Wq': 8.0, 'L0_cond_Wk': 8.0, 'L1_cond_Wk': 4.21}
    for name, (base, spread) in spreads.items():
        noise = np.random.default_rng([zlib.crc32(name.encode()), seed]).standard_normal(out[name].shape)
        drawn = base * np.exp(spread * noise) if base else spread * noise
        out[name] = jnp.asarray(drawn.astype(out[name].dtype))
    for name, factor in factors.items():
        out[name] = (out[name] * factor).astype(out[name].dtype)
    return out
```

```python
from contextlib import ExitStack

import concourse.bass as bass
from concourse import mybir

P = 128
ACT = mybir.ActivationFunctionType
ALU = mybir.AluOpType
F32 = mybir.dt.float32
F16 = mybir.dt.float16
I32 = mybir.dt.int32
AX_X = mybir.AxisListType.X

EPS = 1e-5
Z_SCALE = 256.0
W_SCALE = 64.0
G_SCALE = 64.0
QKV_SCALE = Z_SCALE * W_SCALE
OUT_SCALE = G_SCALE * W_SCALE * 2.0
MASK0 = 1.0e6
MASK1 = 1.0e30
BIG = 3.0e38


class Step:

    def __init__(self, base, front, layer=None):
        self.base, self.front, self.layer = base, front, layer
        self.static = layer is None


class Item:

    def __init__(self, step, back, sequences, layers):
        k = step.front - back
        self.index = step.base + k
        self.parity = k % 2
        self.static = step.static
        self.exists = not step.static or 0 <= k < sequences * layers
        self.layer = k // sequences if step.static else step.layer
        self.sequence = self.index - self.layer * sequences
        self.first_two = step.static and k < 2
        self.starts_layer = step.static and k % sequences == 0
        self.after_layer1 = self.layer == 1 and not self.starts_layer
        self.next_exists = not step.static or k < sequences * layers - 1


def two_layers(nc, x, cond_t, mask0_row, mask1_row, mask0_col, mask1_col, identity, indicators,
               columns, rows, w_in, w_emb, w_out, out):
    B, S, D = x.shape
    L = w_in.shape[0]
    TE = w_emb.shape[1]
    T, C, EC = S // P, D // P, TE // P
    DH = (32, 16)
    HEADS = [D // d for d in DH]
    HC = [P // d for d in DH]
    N = T * D
    LAST = B * L
    assert T == 2 and C == 2 and L == 2 and B % 2 == 0

    x_dram = x.rearrange("b (t p) f -> p b t f", p=P)
    out_dram = out.rearrange("b (t p) f -> p b t f", p=P)
    mask_dram = nc.dram_tensor("mask_rows", (L, B, S), F32, kind="Internal").ap()

    ctx = ExitStack()
    with ctx:
        def sb(name, shape, dt=F32):
            return ctx.enter_context(nc.sbuf_tensor(name, shape, dt))

        def pair(name, shape, dt=F32):
            return [sb(f"{name}{i}", shape, dt) for i in range(2)]

        def bank(name):
            return ctx.enter_context(nc.psum_tensor(name, [P, 512], F32))

        def sem(name):
            return ctx.enter_context(nc.semaphore(name))

        x_all = sb("x_all", [P, B * N])
        ident = sb("ident", [P, P])
        head_ind = sb("head_ind", [P, sum(HC)])
        block_mask = [sb(f"block_mask{l}", [P, P]) for l in range(L)]
        col = sb("col", [P, L * 18])
        w_raw = [sb(f"w_raw{l}", [P, C * 3 * D]) for l in range(L)]
        wo_raw = [sb(f"wo_raw{l}", [P, C * D]) for l in range(L)]
        bo = 2 * D
        wemb = [sb(f"wemb{l}", [P, EC * 2 * D]) for l in range(L)]
        row_b = [sb(f"row_b{l}", [P, 3 * D]) for l in range(L)]
        w_hi = [sb(f"w_hi{l}", [P, C * 3 * D], F16) for l in range(L)]
        w_lo = [sb(f"w_lo{l}", [P, C * 3 * D], F16) for l in range(L)]
        w_tmp = sb("w_tmp", [P, C * 3 * D])
        wo_hi = [sb(f"wo_hi{l}", [P, C * D], F16) for l in range(L)]
        wo_lo = [sb(f"wo_lo{l}", [P, C * D], F16) for l in range(L)]
        ln_b = [sb(f"ln_b{l}", [P, C * P]) for l in range(L)]
        cv = [sb(f"cv{l}", [P, D]) for l in range(L)]
        ck = [sb(f"ck{l}", [P, C]) for l in range(L)]
        bias_hi_lo = [sb(f"bias_hi_lo{l}", [64, 2 * D], F16) for l in range(L)]
        bias_tmp = sb("bias_tmp", [64, 4 * D])
        sel_q = sb("sel_q", [64, P], F16)
        sel_o = sb("sel_o", [64, P], F16)
        cond = sb("cond", [P, EC * B])
        cond_s = sb("cond_s", [P, EC * B])
        cond_t2 = sb("cond_t2", [P, EC * B])
        film = sb("film", [P, 4 * B])
        item_col = [sb(f"item_col{l}", [P, B * 6]) for l in range(L)]
        m0c = sb("m0c", [P, B * T])
        m1c = sb("m1c", [P, B * T], I32)
        m0r = sb("m0r", [B, S])
        m1r = sb("m1r", [B, S], I32)
        m_add = [sb(f"m_add{l}", [B, S]) for l in range(L)]
        neg_half = sb("neg_half", [P, T])

        x_stats, x_mv, x_rstd = pair("x_stats", [P, T * 6]), pair("x_mv", [P, T * 2]), pair("x_rstd", [P, T])
        x_ve, y_ve = pair("x_ve", [P, T]), pair("y_ve", [P, T])
        z, z_hi, z_lo = pair("z", [P, N]), pair("z_hi", [P, N], F16), pair("z_lo", [P, N], F16)
        m_row, k_add = pair("m_row", [P, S]), pair("k_add", [P, C * S])
        k_neg, k_neg_max, k_sum = pair("k_neg", [P, C * S]), pair("k_neg_max", [P, C]), pair("k_sum", [P, C])
        ek, ek_row = pair("ek", [P, C * S]), pair("ek_row", [P, N])
        q_max, q_sub, eq = pair("q_max", [P, T * 16]), pair("q_sub", [P, N]), pair("eq", [P, N])
        eq_t, v = pair("eq_t", [P, C * S]), pair("v", [P, N])
        v_sum = pair("v_sum", [P, T])
        vcol = pair("vcol", [P, T])
        k_rsum, att_s = pair("k_rsum", [P, C]), pair("att_s", [P, C * P])
        att_e = [pair(f"att_e{l}_", [P, C * (P + HC[l])]) for l in range(L)]
        y_rsum, y_n = pair("y_rsum", [P, T * 16]), pair("y_n", [P, N])
        y_stats, y_mv, y_rstd = pair("y_stats", [P, T * 6]), pair("y_mv", [P, T * 2]), pair("y_rstd", [P, T])
        y_nm, y_shift, y_z = pair("y_nm", [P, T]), pair("y_shift", [P, T]), pair("y_z", [P, N])
        icol = pair("icol", [P, 2 * C])
        h, th, g = pair("h", [P, N]), pair("th", [P, N]), pair("g", [P, N])
        g_hi, g_lo = pair("g_hi", [P, N], F16), pair("g_lo", [P, N], F16)

        ps_zk = bank("ps_zk")
        ps_qv = [bank(f"ps_qv{t}") for t in range(T)]
        ps_eo = bank("ps_eo")
        ps_qy = bank("ps_qy")
        ps_att = bank("ps_att")
        ps_y = [bank(f"ps_y{t}") for t in range(T)]

        const_in, cond_in, col_in, mask_in = map(sem, ("const_in", "cond_in", "col_in", "mask_in"))
        w_in_s = [sem(f"w_in{l}") for l in range(L)]
        w_late_in = [sem(f"w_late_in{l}") for l in range(L)]
        x_in = [sem(f"x_in{i}") for i in range(2)]
        m_row_in = [sem(f"m_row_in{i}") for i in range(2)]
        mask_rows_made, mask_rows_out = sem("mask_rows_made"), sem("mask_rows_out")
        ln_b_ready, w_scaled, w_hi_made, w_ready = map(sem, ("ln_b_ready", "w_scaled", "w_hi_made", "w_ready"))
        wo_scaled, wo_hi_made, wo_ready = map(sem, ("wo_scaled", "wo_hi_made", "wo_ready"))
        rows_done, rows_made, rows_scaled, rows_split = map(sem, ("rows_done", "rows_made", "rows_scaled", "rows_split"))
        rows_ready, ck_done, ck_made, ck_ready = map(sem, ("rows_ready", "ck_done", "ck_made", "ck_ready"))
        film_done, film_made, film_mixed, item_col_ready = map(
            sem, ("film_done", "film_made", "film_mixed", "item_col_ready"))
        cond_tanh, cond_silu, vmask_made = map(sem, ("cond_tanh", "cond_silu", "vmask_made"))
        neg_half_made, sel_cleared, sel_made, ind_made, block_mask_made = map(
            sem, ("neg_half_made", "sel_cleared", "sel_made", "ind_made", "block_mask_made"))
        x_bn, x_stats_ready, x_ve_ready, x_rstd_ready, z_ready = map(
            sem, ("x_bn", "x_stats_ready", "x_ve_ready", "x_rstd_ready", "z_ready"))
        zt_done, z_hi_ready, z_lo_ready = map(sem, ("zt_done", "z_hi_ready", "z_lo_ready"))
        k_done, k_add_ready, k_neg_ready, ek_ready = map(sem, ("k_done", "k_add_ready", "k_neg_ready", "ek_ready"))
        qv_done = [sem(f"qv{t}_done") for t in range(T)]
        q_max_ready, q_sub_ready, v_ready, eq_ready = map(sem, ("q_max_ready", "q_sub_ready", "v_ready", "eq_ready"))
        turned_done, ek_row_ready, eq_t_ready = map(sem, ("turned_done", "ek_row_ready", "eq_t_ready"))
        k_rsum_ready, att_done, att_s_ready, att_t_done, att_t_ready = map(
            sem, ("k_rsum_ready", "att_done", "att_s_ready", "att_t_done", "att_t_ready"))
        y_done, y_rsum_ready, y_n_ready, y_bn, y_stats_ready = map(
            sem, ("y_done", "y_rsum_ready", "y_n_ready", "y_bn", "y_stats_ready"))
        y_ve_ready, y_rstd_ready, y_shift_ready, y_z_ready, yzt_done = map(
            sem, ("y_ve_ready", "y_rstd_ready", "y_shift_ready", "y_z_ready", "yzt_done"))
        vcol_ready, icol_ready, h_ready, th_ready, g_ready, g_hi_ready, g_lo_ready = map(
            sem, ("vcol_ready", "icol_ready", "h_ready", "th_ready", "g_ready", "g_hi_ready", "g_lo_ready"))
        o_done, x_new, out_out = map(sem, ("o_done", "x_new", "out_out"))

        block = ctx.enter_context(nc.Block())

        def wait_apart(engine, item, *waits):
            if not item.static:
                for _, value in waits:
                    engine.compute_val(value)
                engine.wait_ge(waits[0][0], 1)
            for semaphore, value in waits:
                engine.wait_ge(semaphore, value)

        def steps(engine, run):
            for front in range(0, 6):
                run(Step(0, front))
            with engine.Fori(6, B - 1, 2) as r:
                for u in range(2):
                    run(Step(r, u, 0))
            for front in range(B, B + 6):
                run(Step(0, front))
            with engine.Fori(B + 6, LAST - 1, 2) as r:
                for u in range(2):
                    run(Step(r, u, 1))
            for front in range(LAST, LAST + 6):
                run(Step(0, front))

        def at(step, back):
            return Item(step, back, B, L)

        def part(tile, i, width=D):
            return tile[:, i * width:(i + 1) * width]

        @block.sync
        def _(sp):
            sp.dma_start(col[:, :], columns).then_inc(col_in, 16)
            sp.dma_start(w_raw[0][:, :].rearrange("p (c n) -> p c n", c=C),
                         w_in[0].rearrange("(c p) n -> p c n", p=P)).then_inc(w_in_s[0], 16)
            sp.dma_start(m0r[:, :], mask0_row).then_inc(mask_in, 16)
            sp.dma_start(m1r[:, :], mask1_row).then_inc(mask_in, 16)
            sp.dma_start(row_b[0][:, :], rows[0].partition_broadcast(P)).then_inc(w_in_s[0], 16)
            sp.wait_ge(mask_rows_made, L)
            for l in range(L):
                sp.dma_start(mask_dram[l], m_add[l][:, :]).then_inc(mask_rows_out, 16)
            sp.wait_ge(mask_rows_out, 16 * L)

            def step(s):
                m, done = at(s, 1), at(s, 5)
                if m.exists:
                    j, p = m.index, m.parity
                    if not m.first_two:
                        sp.wait_ge(k_add_ready, j - 1)
                    row = mask_dram[m.layer, m.sequence] if m.static else mask_dram[m.layer, bass.ds(m.sequence, 1), :].rearrange("a n -> (a n)")
                    sp.dma_start(m_row[p][:, :], row.partition_broadcast(P)).then_inc(m_row_in[p], 16)
                if s.static and s.front == 2:
                    with sp.Fori(2, B - 1, 2) as b:
                        for u in range(2):
                            sp.wait_ge(x_in[u], 8 * b)
                            sp.dma_start(x_all[:, bass.ds((b + u) * N, N)].rearrange("p (a t f) -> p a t f", a=1, t=T),
                                         x_dram[:, bass.ds(b + u, 1)]).then_inc(x_in[u], 16)
                if done.exists and done.layer == 1:
                    sp.wait_ge(x_new, done.index + 1)
                    sp.dma_start(out_dram[:, bass.ds(done.sequence, 1)],
                                 x_all[:, bass.ds(done.sequence * N, N)].rearrange("p (a t f) -> p a t f", a=1, t=T))\
                      .then_inc(out_out, 16)

            steps(sp, step)
            sp.wait_ge(out_out, 16 * B)

        @block.scalar
        def _(act):
            act.dma_start(x_all[:, 0:N].rearrange("p (t f) -> p t f", t=T), x_dram[:, 0]).then_inc(x_in[0], 16)
            act.dma_start(ident[:, :], identity).then_inc(const_in, 16)
            act.dma_start(head_ind[:, :], indicators).then_inc(const_in, 16)
            act.dma_start(x_all[:, N:2 * N].rearrange("p (t f) -> p t f", t=T), x_dram[:, 1]).then_inc(x_in[1], 16)
            act.dma_start(cond[:, :], cond_t).then_inc(cond_in, 16)
            act.dma_start(m0c[:, :], mask0_col).then_inc(cond_in, 16)
            act.dma_start(m1c[:, :], mask1_col).then_inc(cond_in, 16)
            for l in range(L):
                if l:
                    act.dma_start(w_raw[l][:, :].rearrange("p (c n) -> p c n", c=C),
                                  w_in[l].rearrange("(c p) n -> p c n", p=P)).then_inc(w_in_s[l], 16)
                    act.dma_start(row_b[l][:, :], rows[l].partition_broadcast(P)).then_inc(w_in_s[l], 16)
                act.dma_start(wo_raw[l][:, :].rearrange("p (c n) -> p c n", c=C),
                              w_out[l].rearrange("(c p) n -> p c n", p=P)).then_inc(w_late_in[l], 16)
                act.dma_start(wemb[l][:, :].rearrange("p (c n) -> p c n", c=EC),
                              w_emb[l].rearrange("(c p) n -> p c n", p=P)).then_inc(w_late_in[l], 16)
            act.wait_ge(cond_in, 48)
            nc.scalar.activation(cond_t2[:, :], cond[:, :], ACT.Tanh, scale=0.5).then_inc(cond_tanh, 1)

            def z_high(a):
                j, p = a.index, a.parity
                act.wait_ge(zt_done, j + 1)
                if not a.first_two:
                    act.wait_ge(qv_done[T - 1], j - 1)
                nc.scalar.activation(z_hi[p][:, :], ps_zk[:, :], ACT.Copy, scale=Z_SCALE).then_inc(z_hi_ready, 1)

            def exps_turned(a):
                j, p = a.index, a.parity
                act.wait_ge(turned_done, j + 1)
                if not a.first_two:
                    act.wait_ge(y_done, j - 1)
                nc.scalar.activation(ek_row[p][:, :], ps_eo[:, :], ACT.Copy).then_inc(ek_row_ready, 1)
                nc.scalar.activation(eq_t[p][:, :], ps_qy[:, :], ACT.Copy).then_inc(eq_t_ready, 1)

            def exp_k(a):
                j, p = a.index, a.parity
                act.wait_ge(k_neg_ready, j + 1)
                if not a.first_two:
                    act.wait_ge(turned_done, j - 1)
                    act.wait_ge(k_rsum_ready, j - 1)
                for c in range(C):
                    last = nc.scalar.activation(part(ek[p], c), part(k_neg[p], c), ACT.Exp, scale=-1.0,
                                                bias=k_neg_max[p][:, c:c + 1], accum_out=k_sum[p][:, c:c + 1])
                last.then_inc(ek_ready, 1)

            def exp_q(a):
                j, p = a.index, a.parity
                act.wait_ge(q_sub_ready, T * j + T)
                if not a.first_two:
                    act.wait_ge(turned_done, j - 1)
                nc.scalar.activation(eq[p][:, :], q_sub[p][:, :], ACT.Exp, scale=1.0 / QKV_SCALE).then_inc(eq_ready, 1)

            def condition(a):
                j, p = a.index, a.parity
                act.wait_ge(yzt_done, j + 1)
                act.wait_ge(icol_ready, j + 1)
                if not a.first_two:
                    act.wait_ge(g_ready, j - 1)
                for c in range(C):
                    last = nc.scalar.activation(part(h[p], c), part(ps_qy, c), ACT.Identity,
                                                scale=icol[p][:, 2 * c:2 * c + 1], bias=icol[p][:, 2 * c + 1:2 * c + 2])
                last.then_inc(h_ready, 1)
                act.wait_ge(h_ready, j + 1)
                nc.scalar.activation(th[p][:, :], h[p][:, :], ACT.Tanh, scale=0.5).then_inc(th_ready, 1)

            def g_high(a):
                j, p = a.index, a.parity
                act.wait_ge(g_ready, j + 1)
                if not a.first_two:
                    act.wait_ge(o_done, j - 1)
                nc.scalar.activation(g_hi[p][:, :], g[p][:, :], ACT.Copy, scale=G_SCALE).then_inc(g_hi_ready, 1)

            def att_turned(a):
                j, p = a.index, a.parity
                act.wait_ge(att_t_done, j - B + 1)
                dst = att_e[1][p][:, :].rearrange("p (c n) -> p c n", c=C)[:, :, 0:P]
                nc.scalar.activation(dst, ps_att[:, C * P:2 * C * P].rearrange("p (c n) -> p c n", c=C), ACT.Copy)\
                  .then_inc(att_t_ready, 1)

            def step(s):
                tz, pr, aa, o = at(s, 1), at(s, 2), at(s, 3), at(s, 4)
                if aa.exists:
                    exps_turned(aa)
                if pr.exists:
                    exp_k(pr)
                if o.exists:
                    condition(o)
                    g_high(o)
                if aa.exists and aa.layer == 1:
                    att_turned(aa)
                if tz.exists:
                    z_high(tz)
                if pr.exists:
                    exp_q(pr)

            steps(act, step)

        @block.gpsimd
        def _(pool):
            pool.wait_ge(neg_half_made, 1)

            def indicators_in_place():
                pool.wait_ge(const_in, 32)
                first = 0
                for l in range(L):
                    for p in range(2):
                        for c in range(C):
                            base = c * (P + HC[l]) + P
                            last = pool.tensor_copy(att_e[l][p][:, base:base + HC[l]], head_ind[:, first:first + HC[l]])
                    first += HC[l]
                last.then_inc(ind_made, 1)

            def x_scale(a):
                j, p = a.index, a.parity
                pool.wait_ge(x_ve_ready, j + 1)
                if not a.first_two:
                    pool.wait_ge(z_ready, j - 1)
                pool.tensor_tensor(x_rstd[p][:, :], x_ve[p][:, :], neg_half[:, :], ALU.pow).then_inc(x_rstd_ready, 1)

            def k_addend(a):
                j, p = a.index, a.parity
                if a.starts_layer:
                    pool.wait_ge(ck_ready, a.layer + 1)
                free = [] if a.first_two else [(k_neg_ready, j - 1)]
                wait_apart(pool, a, (m_row_in[p], 8 * (j - p) + 16), *free)
                for c in range(C):
                    last = pool.tensor_scalar(part(k_add[p], c), m_row[p][:, :], ck[a.layer][:, c:c + 1], 1.0,
                                              ALU.add, ALU.mult)
                last.then_inc(k_add_ready, 1)

            def v_columns(a):
                j, p = a.index, a.parity
                if a.starts_layer and a.layer == 0:
                    pool.wait_ge(vmask_made, 1)
                if not a.first_two:
                    pool.wait_ge(v_ready, T * (j - 1))
                first = a.sequence * 6 + 2 * C
                pool.tensor_copy(vcol[p][:, :], item_col[a.layer][:, bass.ds(first, T)]).then_inc(vcol_ready, 1)

            def ab_columns(a):
                j, p = a.index, a.parity
                if a.starts_layer:
                    pool.wait_ge(item_col_ready, a.layer + 1)
                if not a.first_two:
                    pool.wait_ge(h_ready, j - 1)
                pool.tensor_copy(icol[p][:, :], item_col[a.layer][:, bass.ds(a.sequence * 6, 2 * C)])\
                    .then_inc(icol_ready, 1)

            def y_normalise(a):
                j, p = a.index, a.parity
                pool.wait_ge(y_ve_ready, j + 1)
                if not a.first_two:
                    pool.wait_ge(yzt_done, j - 1)
                pool.tensor_tensor(y_rstd[p][:, :], y_ve[p][:, :], neg_half[:, :], ALU.pow).then_inc(y_rstd_ready, 1)
                pool.wait_ge(y_rstd_ready, j + 1)
                pool.tensor_tensor(y_shift[p][:, :], y_nm[p][:, :], y_rstd[p][:, :], ALU.mult).then_inc(y_shift_ready, 1)
                wait_apart(pool, a, (y_shift_ready, j + 1))
                for t in range(T):
                    last = pool.tensor_scalar(part(y_z[p], t), part(y_n[p], t), y_rstd[p][:, t:t + 1],
                                              y_shift[p][:, t:t + 1], ALU.mult, ALU.add)
                last.then_inc(y_z_ready, 1)

            def step(s):
                f, m, nm = at(s, 0), at(s, 1), at(s, 3)
                if f.exists:
                    x_scale(f)
                if m.exists:
                    k_addend(m)
                    v_columns(m)
                if s.static and s.front == 1:
                    indicators_in_place()
                if nm.exists:
                    ab_columns(nm)
                    y_normalise(nm)

            steps(pool, step)

        @block.vector
        def _(dve):
            vec = nc.vector

            def constants():
                vec.memset(neg_half[:, :], -0.5).then_inc(neg_half_made, 1)
                vec.memset(sel_q[:, :], 0.0)
                vec.memset(sel_o[:, :], 0.0).then_inc(sel_cleared, 1)
                dve.wait_ge(sel_cleared, 1)
                for r in (0, 32):
                    vec.memset(sel_q[r:r + 1, :], Z_SCALE)
                    last = vec.memset(sel_o[r:r + 1, :], 2.0 * G_SCALE)
                last.then_inc(sel_made, 1)

            def mask_rows():
                dve.wait_ge(mask_in, 32)
                vec.tensor_scalar(m_add[0][:, :], m0r[:, :], -1.0, MASK0 * QKV_SCALE, ALU.add, ALU.mult)\
                   .then_inc(mask_rows_made, 1)
                vec.tensor_scalar(m_add[1][:, :], m1r[:, :], 1.0, -MASK1, ALU.is_equal, ALU.mult)\
                   .then_inc(mask_rows_made, 1)

            def block_masks():
                dve.wait_ge(const_in, 32)
                first = 0
                for l in range(L):
                    last = vec.tensor_copy(block_mask[l][:, :].rearrange("p (h d) -> p h d", d=DH[l]),
                                           head_ind[:, first:first + HC[l]].unsqueeze(2).to_broadcast([P, HC[l], DH[l]]))
                    first += HC[l]
                last.then_inc(block_mask_made, 1)

            def value_masks():
                dve.wait_ge(cond_in, 48)
                for t in range(T):
                    it = [item_col[l][:, :].rearrange("p (b k) -> p k b", k=6)[:, 2 * C + t, :] for l in range(L)]
                    vec.tensor_scalar(it[0], m0c[:, t * B:(t + 1) * B], 1.0 / QKV_SCALE, None, ALU.mult)
                    last = vec.tensor_scalar(it[1], m1c[:, t * B:(t + 1) * B], 1.0, 1.0 / QKV_SCALE,
                                             ALU.not_equal, ALU.mult)
                last.then_inc(vmask_made, 1)

            def ln_bias(l):
                dve.wait_ge(col_in, 16)
                for c in range(C):
                    b = col[:, 18 * l + 2 + c:18 * l + 3 + c]
                    last = vec.tensor_copy(ln_b[l][:, c * P:(c + 1) * P], b.to_broadcast([P, P]))
                last.then_inc(ln_b_ready, 1)

            def layer_weights(l):
                dve.wait_ge(w_in_s[l], 32)
                if l:
                    dve.wait_ge(wo_ready, l)
                W = 3 * D
                for c in range(C):
                    last = vec.tensor_scalar(w_tmp[:, c * W:(c + 1) * W], w_raw[l][:, c * W:(c + 1) * W],
                                             col[:, 18 * l + c:18 * l + c + 1], W_SCALE, ALU.mult, ALU.mult)
                last.then_inc(w_scaled, 1)
                dve.wait_ge(w_scaled, l + 1)
                vec.tensor_copy(w_hi[l][:, :], w_tmp[:, :]).then_inc(w_hi_made, 1)
                dve.wait_ge(w_hi_made, l + 1)
                vec.tensor_tensor(w_lo[l][:, :], w_tmp[:, :], w_hi[l][:, :], ALU.subtract).then_inc(w_ready, 1)

            def out_weights(l):
                dve.wait_ge(w_late_in[l], 32)
                dve.wait_ge(w_ready, l + 1)
                vec.tensor_scalar(w_tmp[:, 0:C * D], wo_raw[l][:, :], W_SCALE, None, ALU.mult).then_inc(wo_scaled, 1)
                dve.wait_ge(wo_scaled, l + 1)
                vec.tensor_copy(wo_hi[l][:, :], w_tmp[:, 0:C * D]).then_inc(wo_hi_made, 1)
                dve.wait_ge(wo_hi_made, l + 1)
                vec.tensor_tensor(wo_lo[l][:, :], w_tmp[:, 0:C * D], wo_hi[l][:, :], ALU.subtract).then_inc(wo_ready, 1)

            def k_bias(l, bank):
                dve.wait_ge(ck_done, l + 1)
                vec.tensor_tensor(ck[l][:, :], bank[:, 0:C], col[:, 18 * l + 4:18 * l + 6], ALU.add).then_inc(ck_made, 1)
                dve.wait_ge(ck_made, l + 1)
                vec.tensor_scalar(ck[l][:, :], ck[l][:, :], QKV_SCALE, None, ALU.mult).then_inc(ck_ready, 1)

            def row_biases(l, bank):
                dve.wait_ge(rows_done, l + 1)
                if l:
                    dve.wait_ge(rows_ready, l)
                vec.tensor_tensor(cv[l][:, :], bank[:, D:2 * D], row_b[l][:, D:2 * D], ALU.add)
                vec.tensor_tensor(bias_tmp[:, 0:D], bank[0:64, 0:D], row_b[l][0:64, 0:D], ALU.add).then_inc(rows_made, 1)
                dve.wait_ge(rows_made, l + 1)
                vec.tensor_scalar(cv[l][:, :], cv[l][:, :], QKV_SCALE, None, ALU.mult)
                vec.tensor_scalar(bias_tmp[:, D:2 * D], bias_tmp[:, 0:D], W_SCALE, None, ALU.mult)
                vec.tensor_scalar(bias_tmp[:, 2 * D:3 * D], row_b[l][0:64, bo:bo + D], W_SCALE, None, ALU.mult)\
                   .then_inc(rows_scaled, 1)
                dve.wait_ge(rows_scaled, l + 1)
                vec.tensor_copy(bias_hi_lo[l][:, :], bias_tmp[:, D:3 * D]).then_inc(rows_split, 1)
                dve.wait_ge(rows_split, l + 1)
                vec.tensor_tensor(bias_hi_lo[l][32:64, :], bias_tmp[32:64, D:3 * D], bias_hi_lo[l][32:64, :],
                                  ALU.subtract).then_inc(rows_ready, 1)

            def silu_cond():
                dve.wait_ge(cond_tanh, 1)
                vec.scalar_tensor_tensor(cond_s[:, :], cond_t2[:, :], 1.0, cond[:, :], ALU.add, ALU.mult)\
                   .then_inc(cond_silu, 1)

            def film_columns(l, bank, first):
                base = 18 * l
                dve.wait_ge(film_done, l + 1)
                if l:
                    dve.wait_ge(item_col_ready, l)
                for e in range(2 * C):
                    last = vec.tensor_scalar(film[:, e * B:(e + 1) * B], bank[:, first + e * B:first + (e + 1) * B], 0.5,
                                             col[:, base + 6 + e:base + 7 + e], ALU.mult, ALU.add)
                last.then_inc(film_made, 1)
                dve.wait_ge(film_made, l + 1)
                it = item_col[l][:, :].rearrange("p (b k) -> p k b", k=6)
                for c in range(C):
                    l2w, l2b = col[:, base + 10 + c:base + 11 + c], col[:, base + 12 + c:base + 13 + c]
                    vec.tensor_scalar(it[:, 2 * c, :], film[:, c * B:(c + 1) * B], 1.0, l2w, ALU.add, ALU.mult)
                    last = vec.tensor_scalar(it[:, 2 * c + 1, :], film[:, c * B:(c + 1) * B], 1.0, l2b, ALU.add, ALU.mult)
                last.then_inc(film_mixed, 1)
                dve.wait_ge(film_mixed, l + 1)
                for c in range(C):
                    last = vec.tensor_tensor(it[:, 2 * c + 1, :], it[:, 2 * c + 1, :],
                                             film[:, (C + c) * B:(C + c + 1) * B], ALU.add)
                last.then_inc(item_col_ready, 1)

            def stats(a):
                j, p = a.index, a.parity
                if a.layer == 0:
                    dve.wait_ge(x_in[p], 8 * (j - p) + 16)
                else:
                    dve.wait_ge(x_new, j - B + 1)
                for t in range(T):
                    last = vec.bn_stats(x_stats[p][:, 6 * t:6 * t + 6], x_all[:, bass.ds(a.sequence * N + t * D, D)])
                last.then_inc(x_bn, 1)
                wait_apart(dve, a, (x_bn, j + 1))
                for t in range(T):
                    last = vec.bn_aggr(x_mv[p][:, 2 * t:2 * t + 2], x_stats[p][:, 6 * t:6 * t + 6])
                last.then_inc(x_stats_ready, 1)
                dve.wait_ge(x_stats_ready, j + 1)
                vec.tensor_scalar(x_ve[p][:, :], x_mv[p][:, 1:2 * T:2], EPS, None, ALU.add).then_inc(x_ve_ready, 1)

            def normalise(a):
                j, p = a.index, a.parity
                dve.wait_ge(x_rstd_ready, j + 1)
                if not a.first_two:
                    dve.wait_ge(zt_done, j - 1)
                for t in range(T):
                    last = vec.tensor_scalar(part(z[p], t), x_all[:, bass.ds(a.sequence * N + t * D, D)],
                                             x_mv[p][:, 2 * t:2 * t + 1], x_rstd[p][:, t:t + 1],
                                             ALU.subtract, ALU.mult)
                last.then_inc(z_ready, 1)

            def z_low(a):
                j, p = a.index, a.parity
                dve.wait_ge(z_hi_ready, j + 1)
                vec.scalar_tensor_tensor(z_lo[p][:, :], ps_zk[:, :], Z_SCALE, z_hi[p][:, :], ALU.mult, ALU.subtract)\
                   .then_inc(z_lo_ready, 1)

            def k_shift(a):
                j, p = a.index, a.parity
                free = [] if a.first_two else [(ek_ready, j - 1)]
                wait_apart(dve, a, (k_done, j + 1), (k_add_ready, j + 1), *free)
                for c in range(C):
                    last = vec.tensor_tensor_reduce(out=part(k_neg[p], c), in0=part(ps_zk, c), in1=part(k_add[p], c),
                                                    scale=-1.0 / QKV_SCALE, scalar=BIG, op0=ALU.add, op1=ALU.min,
                                                    accum_out=k_neg_max[p][:, c:c + 1])
                last.then_inc(k_neg_ready, 1)

            def q_shift_and_v(a, t):
                j, p, l = a.index, a.parity, a.layer
                dve.wait_ge(qv_done[t], j + 1)
                if t == 0:
                    dve.wait_ge(vcol_ready, j + 1)
                    if not a.first_two:
                        dve.wait_ge(eq_ready, j - 1)
                        dve.wait_ge(att_done, j - 1)
                q = ps_qv[t][:, 0:D].rearrange("p (h d) -> p h d", d=DH[l])
                q_m = q_max[p][:, t * 16:t * 16 + HEADS[l]]
                vec.tensor_reduce(q_m, q, AX_X, ALU.max).then_inc(q_max_ready, 1)
                vec.tensor_tensor_reduce(out=part(v[p], t), in0=ps_qv[t][:, D:2 * D], in1=cv[l][:, :],
                                         scale=vcol[p][:, t:t + 1], scalar=0.0, op0=ALU.add, op1=ALU.add,
                                         accum_out=v_sum[p][:, t:t + 1]).then_inc(v_ready, 1)
                dve.wait_ge(q_max_ready, T * j + t + 1)
                vec.tensor_tensor(part(q_sub[p], t).rearrange("p (h d) -> p h d", d=DH[l]), q,
                                  q_m.unsqueeze(2).to_broadcast([P, HEADS[l], DH[l]]), ALU.subtract)\
                   .then_inc(q_sub_ready, 1)

            def att_scale(a):
                j, p, l = a.index, a.parity, a.layer
                dve.wait_ge(ek_ready, j + 1)
                vec.reciprocal(k_rsum[p][:, :], k_sum[p][:, :]).then_inc(k_rsum_ready, 1)
                dve.wait_ge(k_rsum_ready, j + 1)
                dve.wait_ge(att_done, j + 1)
                if not a.first_two:
                    dve.wait_ge(y_done, j - 1)
                for c in range(C):
                    base = c * (P + HC[l])
                    dst = att_e[l][p][:, base:base + P] if l == 0 else part(att_s[p], c, P)
                    last = vec.scalar_tensor_tensor(dst, part(ps_att, c, P), k_rsum[p][:, c:c + 1],
                                                    block_mask[l][:, :], ALU.mult, ALU.mult)
                last.then_inc(att_s_ready, 1)

            def y_divide(a):
                j, p, l = a.index, a.parity, a.layer
                W = P + HC[l]
                dve.wait_ge(y_done, j + 1)
                r = [y_rsum[p][:, t * 16:t * 16 + HEADS[l]].rearrange("p (c n) -> p c n", c=C) for t in range(T)]
                y = [ps_y[t][:, 0:C * W].rearrange("p (c n) -> p c n", c=C) for t in range(T)]
                for t in range(T):
                    last = vec.reciprocal(r[t], y[t][:, :, P:W])
                last.then_inc(y_rsum_ready, 1)
                dve.wait_ge(y_rsum_ready, j + 1)
                if not a.first_two:
                    dve.wait_ge(y_z_ready, j - 1)
                for t in range(T):
                    last = vec.tensor_tensor(part(y_n[p], t).rearrange("p (c h d) -> p c h d", c=C, d=DH[l]),
                                             y[t][:, :, 0:P].rearrange("p c (h d) -> p c h d", d=DH[l]),
                                             r[t].unsqueeze(3).to_broadcast([P, C, HC[l], DH[l]]), ALU.mult)
                last.then_inc(y_n_ready, 1)

            def y_statistics(a):
                j, p = a.index, a.parity
                dve.wait_ge(y_n_ready, j + 1)
                for t in range(T):
                    last = vec.bn_stats(y_stats[p][:, 6 * t:6 * t + 6], part(y_n[p], t))
                last.then_inc(y_bn, 1)
                wait_apart(dve, a, (y_bn, j + 1))
                for t in range(T):
                    last = vec.bn_aggr(y_mv[p][:, 2 * t:2 * t + 2], y_stats[p][:, 6 * t:6 * t + 6])
                last.then_inc(y_stats_ready, 1)
                dve.wait_ge(y_stats_ready, j + 1)
                vec.tensor_scalar(y_nm[p][:, :], y_mv[p][:, 0:2 * T:2], -1.0, None, ALU.mult)
                vec.tensor_scalar(y_ve[p][:, :], y_mv[p][:, 1:2 * T:2], EPS, None, ALU.add).then_inc(y_ve_ready, 1)

            def gate(a):
                j, p = a.index, a.parity
                dve.wait_ge(th_ready, j + 1)
                vec.scalar_tensor_tensor(g[p][:, :], th[p][:, :], 1.0, h[p][:, :], ALU.add, ALU.mult).then_inc(g_ready, 1)

            def g_low(a):
                j, p = a.index, a.parity
                dve.wait_ge(g_hi_ready, j + 1)
                vec.scalar_tensor_tensor(g_lo[p][:, :], g[p][:, :], G_SCALE, g_hi[p][:, :], ALU.mult, ALU.subtract)\
                   .then_inc(g_lo_ready, 1)

            def residual(a):
                j = a.index
                dve.wait_ge(o_done, j + 1)
                xs = x_all[:, bass.ds(a.sequence * N, N)]
                vec.scalar_tensor_tensor(xs, ps_eo[:, :], 1.0 / OUT_SCALE, xs, ALU.mult, ALU.add).then_inc(x_new, 1)

            constants()
            ln_bias(0)
            mask_rows()
            layer_weights(0)

            def step(s):
                f, tz, pr, aa, o, done = (at(s, back) for back in range(6))
                if done.exists:
                    residual(done)
                if pr.exists:
                    k_shift(pr)
                if f.exists:
                    stats(f)
                if s.static and s.front == 0:
                    k_bias(0, ps_y[0])
                    row_biases(0, ps_att)
                    block_masks()
                    value_masks()
                if pr.exists:
                    q_shift_and_v(pr, 0)
                if aa.exists:
                    att_scale(aa)
                if o.exists:
                    gate(o)
                    g_low(o)
                if pr.exists:
                    q_shift_and_v(pr, 1)
                if f.exists:
                    normalise(f)
                if tz.exists:
                    z_low(tz)
                if aa.exists:
                    y_divide(aa)
                    y_statistics(aa)
                if s.static and s.front == 2:
                    silu_cond()
                    out_weights(0)
                    film_columns(0, ps_y[0], 0)
                if s.static and s.front == 3:
                    layer_weights(1)
                    ln_bias(1)
                if s.static and s.front == 4:
                    row_biases(1, ps_att)
                if s.static and s.front == 5:
                    k_bias(1, ps_att)
                    out_weights(1)
                    film_columns(1, ps_att, 64)

            steps(dve, step)

        @block.tensor
        def _(pe):
            mm, turn = nc.tensor.matmul, nc.tensor.transpose
            W = 3 * D

            def row_bias_products(l, bank):
                pe.wait_ge(w_in_s[l], 32)
                pe.wait_ge(ln_b_ready, l + 1)
                if l:
                    pe.wait_ge(att_s_ready, 2)
                for c in range(C):
                    last = mm(bank[:, :], ln_b[l][:, c * P:(c + 1) * P], w_raw[l][:, c * W + D:(c + 1) * W],
                              start=(c == 0), stop=(c == C - 1))
                last.then_inc(rows_done, 1)

            def k_bias_products(l, bank):
                if l:
                    pe.wait_ge(rows_ready, l + 1)
                    pe.wait_ge(att_s_ready, 3)
                for d in range(C):
                    for c in range(C):
                        last = mm(bank[:, d:d + 1], w_raw[l][:, c * W + d * P:c * W + (d + 1) * P],
                                  ln_b[l][:, c * P:c * P + 1], start=(c == 0), stop=(c == C - 1))
                last.then_inc(ck_done, 1)

            def film_products(l, bank, first):
                pe.wait_ge(w_late_in[l], 32)
                pe.wait_ge(cond_silu, 1)
                pe.wait_ge(ck_made, l + 1)
                for e in range(2 * C):
                    for c in range(EC):
                        last = mm(bank[:, first + e * B:first + (e + 1) * B],
                                  wemb[l][:, c * 2 * D + e * P:c * 2 * D + (e + 1) * P],
                                  cond_s[:, c * B:(c + 1) * B], start=(c == 0), stop=(c == EC - 1))
                last.then_inc(film_done, 1)

            def turn_z(a):
                j, p = a.index, a.parity
                pe.wait_ge(z_ready, j + 1)
                if not (a.static and a.index == 0):
                    pe.wait_ge(k_neg_ready, j)
                for c in range(C):
                    for t in range(T):
                        last = turn(ps_zk[:, c * S + t * P:c * S + (t + 1) * P],
                                    z[p][:, t * D + c * P:t * D + (c + 1) * P], ident[:, :])
                last.then_inc(zt_done, 1)

            def project_k(a):
                j, p, l = a.index, a.parity, a.layer
                pe.wait_ge(z_lo_ready, j + 1)
                if a.starts_layer:
                    pe.wait_ge(w_ready, l + 1)
                for d in range(C):
                    n = 0
                    for c in range(C):
                        for w, zz in ((w_hi, z_hi), (w_hi, z_lo), (w_lo, z_hi)):
                            last = mm(part(ps_zk, d), w[l][:, c * W + d * P:c * W + (d + 1) * P], part(zz[p], c),
                                      start=(n == 0), stop=(n == 3 * C - 1))
                            n += 1
                last.then_inc(k_done, 1)

            def project_qv(a, t):
                j, p, l = a.index, a.parity, a.layer
                if a.starts_layer and t == 0:
                    pe.wait_ge(rows_ready, l + 1)
                    pe.wait_ge(sel_made, 1)
                if not (a.static and a.index == 0):
                    pe.wait_ge(q_sub_ready, T * (j - 1) + t + 1)
                n = 0
                for c in range(C):
                    for zz, w in ((z_hi, w_hi), (z_hi, w_lo), (z_lo, w_hi)):
                        last = mm(ps_qv[t][:, :], zz[p][:, c * S + t * P:c * S + (t + 1) * P], w[l][:, c * W + D:(c + 1) * W],
                           start=(n == 0), stop=(n == 3 * C - 1))
                        if n == 0:
                            mm(ps_qv[t][:, 0:D], sel_q[:, :], bias_hi_lo[l][:, 0:D], start=False, stop=False)
                        n += 1
                last.then_inc(qv_done[t], 1)

            def turn_exps(a):
                j, p = a.index, a.parity
                pe.wait_ge(ek_ready, j + 1)
                if not a.first_two:
                    pe.wait_ge(x_new, j - 1)
                for t in range(T):
                    for c in range(C):
                        turn(ps_eo[:, t * D + c * P:t * D + (c + 1) * P],
                             ek[p][:, c * S + t * P:c * S + (t + 1) * P], ident[:, :])
                pe.wait_ge(eq_ready, j + 1)
                if not a.first_two:
                    pe.wait_ge(h_ready, j - 1)
                for c in range(C):
                    for t in range(T):
                        last = turn(ps_qy[:, c * S + t * P:c * S + (t + 1) * P],
                                    eq[p][:, t * D + c * P:t * D + (c + 1) * P], ident[:, :])
                last.then_inc(turned_done, 1)

            def attend(a):
                j, p, l = a.index, a.parity, a.layer
                pe.wait_ge(ek_row_ready, j + 1)
                pe.wait_ge(v_ready, T * j + T)
                if a.static and a.index == 0:
                    pe.wait_ge(rows_ready, 1)
                elif a.static and a.index == 2:
                    pe.wait_ge(rows_ready, 2)
                elif a.static and a.index == 3:
                    pe.wait_ge(item_col_ready, 2)
                if not (a.static and a.index == 0):
                    if a.after_layer1:
                        pe.wait_ge(att_t_ready, j - B)
                    else:
                        pe.wait_ge(att_s_ready, j)
                for c in range(C):
                    for t in range(T):
                        last = mm(part(ps_att, c, P), ek_row[p][:, t * D + c * P:t * D + (c + 1) * P],
                                  v[p][:, t * D + c * P:t * D + (c + 1) * P], start=(t == 0), stop=(t == T - 1))
                last.then_inc(att_done, 1)

            def turn_att(a):
                j, p = a.index, a.parity
                pe.wait_ge(att_s_ready, j + 1)
                for c in range(C):
                    last = turn(part(ps_att, C + c, P), part(att_s[p], c, P), ident[:, :])
                last.then_inc(att_t_done, 1)

            def attention_out(a):
                j, p, l = a.index, a.parity, a.layer
                E = P + HC[l]
                pe.wait_ge(eq_t_ready, j + 1)
                if l == 0:
                    pe.wait_ge(att_s_ready, j + 1)
                else:
                    pe.wait_ge(att_t_ready, j - B + 1)
                if a.static and a.index == 0:
                    pe.wait_ge(ind_made, 1)
                    pe.wait_ge(film_made, 1)
                else:
                    pe.wait_ge(y_n_ready, j)
                for t in range(T):
                    for c in range(C):
                        last = mm(part(ps_y[t], c, E), eq_t[p][:, c * S + t * P:c * S + (t + 1) * P],
                                  part(att_e[l][p], c, E), start=True, stop=True)
                last.then_inc(y_done, 1)

            def turn_y(a):
                j, p = a.index, a.parity
                pe.wait_ge(y_z_ready, j + 1)
                if a.next_exists:
                    pe.wait_ge(eq_t_ready, j + 2)
                for c in range(C):
                    for t in range(T):
                        last = turn(ps_qy[:, c * S + t * P:c * S + (t + 1) * P],
                                    y_z[p][:, t * D + c * P:t * D + (c + 1) * P], ident[:, :])
                last.then_inc(yzt_done, 1)

            def project_out(a):
                j, p, l = a.index, a.parity, a.layer
                pe.wait_ge(g_lo_ready, j + 1)
                if a.starts_layer:
                    pe.wait_ge(wo_ready, l + 1)
                if a.next_exists:
                    pe.wait_ge(ek_row_ready, j + 2)
                for t in range(T):
                    n = 0
                    for c in range(C):
                        for gg, w in ((g_hi, wo_hi), (g_hi, wo_lo), (g_lo, wo_hi)):
                            mm(part(ps_eo, t), gg[p][:, c * S + t * P:c * S + (t + 1) * P], part(w[l], c),
                               start=(n == 0), stop=False)
                            n += 1
                    last = mm(part(ps_eo, t), sel_o[:, :], bias_hi_lo[l][:, D:2 * D], start=False, stop=True)
                last.then_inc(o_done, 1)

            row_bias_products(0, ps_att)
            k_bias_products(0, ps_y[0])
            pe.wait_ge(const_in, 32)

            def step(s):
                tz, pr, aa, o = (at(s, back) for back in range(1, 5))
                if pr.exists:
                    project_k(pr)
                if aa.exists:
                    turn_exps(aa)
                if pr.exists:
                    project_qv(pr, 0)
                if o.exists:
                    turn_y(o)
                if aa.exists:
                    attend(aa)
                if pr.exists:
                    project_qv(pr, 1)
                if aa.exists and aa.layer == 1:
                    turn_att(aa)
                if tz.exists:
                    turn_z(tz)
                if s.static and s.front == 2:
                    film_products(0, ps_y[0], 0)
                if aa.exists:
                    attention_out(aa)
                if o.exists:
                    project_out(o)
                if s.static and s.front == 4:
                    row_bias_products(1, ps_att)
                if s.static and s.front == 5:
                    k_bias_products(1, ps_att)
                    film_products(1, ps_att, 64)

            steps(pe, step)


def kernel(**inputs):
    import numpy as np
    import concourse.bacc as bacc
    from concourse.bass_utils import run_bass_kernel_spmd as run

    f = {n: np.asarray(a) for n, a in inputs.items()}
    P, B, S = 128, f["x"].shape[0], f["x"].shape[1]
    names = [dict(lw="L0_cond_ln_w", lb="L0_cond_ln_b", q="L0_cond_Wq", bq="L0_cond_bq", k="L0_cond_Wk", bk="L0_cond_bk",
                  v="L0_cond_Wv", bv="L0_cond_bv", e="L0_cond_W_emb", be="L0_cond_b_emb", l2w="L0_cond_ln2_w",
                  l2b="L0_cond_ln2_b", o="L0_cond_W_out", bo="L0_cond_b_out"),
             dict(lw="L1_cond_norm_scale", lb="L1_cond_norm_bias", q="L1_cond_Wq", bq="L1_cond_bq", k="L1_cond_Wk",
                  bk="L1_cond_bk", v="L1_cond_Wv", bv="L1_cond_bv", e="L1_cond_film_emb_W", be="L1_cond_film_emb_b",
                  l2w="L1_cond_film_norm_scale", l2b="L1_cond_film_norm_bias", o="L1_cond_film_out_W",
                  bo="L1_cond_film_out_b")]

    def column(a):
        return a.reshape(-1, P).T

    def head_indicators():
        return np.concatenate([np.arange(P)[:, None] // d == np.arange(P // d)[None, :] for d in (32, 16)], 1)

    arrays = {
        "x": f["x"],
        "cond_t": f["cond_2048"].T.reshape(-1, P, B).transpose(1, 0, 2).reshape(P, -1),
        "mask0_row": f["mask_BxSx1_fk1"].reshape(B, S),
        "mask1_row": f["mask_BxS_ik0"],
        "mask0_col": f["mask_BxSx1_fk1"].reshape(B, S // P, P).transpose(2, 1, 0).reshape(P, -1),
        "mask1_col": f["mask_BxS_ik0"].reshape(B, S // P, P).transpose(2, 1, 0).reshape(P, -1),
        "identity": np.eye(P, dtype=np.float32),
        "indicators": head_indicators().astype(np.float32),
        "columns": np.concatenate([np.concatenate([column(f[n[i]]) for i in ("lw", "lb", "bk", "be", "l2w", "l2b")]
                                                  + [np.zeros((P, 4), np.float32)], 1) for n in names], 1),
        "rows": np.stack([np.concatenate([f[n[i]] for i in ("bq", "bv", "bo")]) for n in names]),
        "w_in": np.stack([np.concatenate([f[n[i]] for i in ("k", "q", "v")], 1) for n in names]),
        "w_emb": np.stack([f[n["e"]] for n in names]),
        "w_out": np.stack([f[n["o"]] for n in names]),
    }
    arrays = {n: np.ascontiguousarray(a) for n, a in arrays.items()}
    nc = bacc.Bacc("TRN2", target_bir_lowering=False, num_devices=1)
    aps = {n: nc.dram_tensor(f"in_{n}", a.shape, mybir.dt.from_np(a.dtype), kind="ExternalInput").ap()
           for n, a in arrays.items()}
    out = nc.dram_tensor("out_0", f["x"].shape, F32, kind="ExternalOutput").ap()
    two_layers(nc, out=out, **aps)
    r = run(nc, [{f"in_{n}": a for n, a in arrays.items()}], core_ids=[0])
    return r.results[0]["out_0"]
```

```python
from contextlib import ExitStack

import concourse.bass as bass
from concourse import mybir

P = 128
ACT = mybir.ActivationFunctionType
ALU = mybir.AluOpType
F32 = mybir.dt.float32
F16 = mybir.dt.float16
I32 = mybir.dt.int32
AX_X = mybir.AxisListType.X

EPS = 1e-5
Z_SCALE = 256.0
W_SCALE = 64.0
G_SCALE = 64.0
QKV_SCALE = Z_SCALE * W_SCALE
OUT_SCALE = G_SCALE * W_SCALE * 2.0
MASK0 = 1.0e6
MASK1 = 1.0e30
BIG = 3.0e38


class Step:

    def __init__(self, base, front, layer=None):
        self.base, self.front, self.layer = base, front, layer
        self.static = layer is None


class Item:

    def __init__(self, step, back, sequences, layers):
        k = step.front - back
        self.index = step.base + k
        self.parity = k % 2
        self.static = step.static
        self.exists = not step.static or 0 <= k < sequences * layers
        self.layer = k // sequences if step.static else step.layer
        self.sequence = self.index - self.layer * sequences
        self.first_two = step.static and k < 2
        self.starts_layer = step.static and k % sequences == 0
        self.after_layer1 = self.layer == 1 and not self.starts_layer
        self.next_exists = not step.static or k < sequences * layers - 1


def two_layers(nc, x, cond_t, mask0_row, mask1_row, mask0_col, mask1_col, identity, indicators,
               columns, rows, w_in, w_emb, w_out, out):
    B, S, D = x.shape
    L = w_in.shape[0]
    TE = w_emb.shape[1]
    T, C, EC = S // P, D // P, TE // P
    DH = (32, 16)
    HEADS = [D // d for d in DH]
    HC = [P // d for d in DH]
    N = T * D
    LAST = B * L
    assert T == 2 and C == 2 and L == 2 and B % 2 == 0

    x_dram = x.rearrange("b (t p) f -> p b t f", p=P)
    out_dram = out.rearrange("b (t p) f -> p b t f", p=P)
    mask_dram = nc.dram_tensor("mask_rows", (L, B, S), F32, kind="Internal").ap()

    ctx = ExitStack()
    with ctx:
        def sb(name, shape, dt=F32):
            return ctx.enter_context(nc.sbuf_tensor(name, shape, dt))

        def pair(name, shape, dt=F32):
            return [sb(f"{name}{i}", shape, dt) for i in range(2)]

        def bank(name):
            return ctx.enter_context(nc.psum_tensor(name, [P, 512], F32))

        def sem(name):
            return ctx.enter_context(nc.semaphore(name))

        x_all = sb("x_all", [P, B * N])
        ident = sb("ident", [P, P])
        head_ind = sb("head_ind", [P, sum(HC)])
        block_mask = [sb(f"block_mask{l}", [P, P]) for l in range(L)]
        col = sb("col", [P, L * 18])
        w_raw = [sb(f"w_raw{l}", [P, C * 3 * D]) for l in range(L)]
        wo_raw = [sb(f"wo_raw{l}", [P, C * D]) for l in range(L)]
        bo = 2 * D
        wemb = [sb(f"wemb{l}", [P, EC * 2 * D]) for l in range(L)]
        row_b = [sb(f"row_b{l}", [P, 3 * D]) for l in range(L)]
        w_hi = [sb(f"w_hi{l}", [P, C * 3 * D], F16) for l in range(L)]
        w_lo = [sb(f"w_lo{l}", [P, C * 3 * D], F16) for l in range(L)]
        w_tmp = sb("w_tmp", [P, C * 3 * D])
        wo_hi = [sb(f"wo_hi{l}", [P, C * D], F16) for l in range(L)]
        wo_lo = [sb(f"wo_lo{l}", [P, C * D], F16) for l in range(L)]
        ln_b = [sb(f"ln_b{l}", [P, C * P]) for l in range(L)]
        ck = [sb(f"ck{l}", [P, C]) for l in range(L)]
        bias_hi_lo = [sb(f"bias_hi_lo{l}", [64, 3 * D], F16) for l in range(L)]
        bias_row, bias_tmp = sb("bias_row", [64, 3 * D]), sb("bias_tmp", [64, 3 * D])
        sel_q = sb("sel_q", [64, P], F16)
        sel_o = sb("sel_o", [64, P], F16)
        cond = sb("cond", [P, EC * B])
        cond_s = sb("cond_s", [P, EC * B])
        cond_t2 = sb("cond_t2", [P, EC * B])
        film = sb("film", [P, 4 * B])
        item_col = [sb(f"item_col{l}", [P, B * 6]) for l in range(L)]
        m0c = sb("m0c", [P, B * T])
        m1c = sb("m1c", [P, B * T], I32)
        m0r = sb("m0r", [B, S])
        m1r = sb("m1r", [B, S], I32)
        m_add = [sb(f"m_add{l}", [B, S]) for l in range(L)]
        neg_half = sb("neg_half", [P, T])

        x_stats, x_mv, x_rstd = pair("x_stats", [P, T * 6]), pair("x_mv", [P, T * 2]), pair("x_rstd", [P, T])
        x_ve, y_ve, x_nm, x_shift = (pair(n, [P, T]) for n in ("x_ve", "y_ve", "x_nm", "x_shift"))
        z, z_hi, z_lo = pair("z", [P, N]), pair("z_hi", [P, N], F16), pair("z_lo", [P, N], F16)
        m_row, k_add = pair("m_row", [P, S]), pair("k_add", [P, C * S])
        k_neg, k_neg_max, k_sum = pair("k_neg", [P, C * S]), pair("k_neg_max", [P, C]), pair("k_sum", [P, C])
        ek, ek_row = pair("ek", [P, C * S]), pair("ek_row", [P, N])
        q_max, q_sub, eq = pair("q_max", [P, T * 16]), pair("q_sub", [P, N]), pair("eq", [P, N])
        eq_t, v = pair("eq_t", [P, C * S]), pair("v", [P, N])
        vcol = pair("vcol", [P, T])
        k_rsum, att_s = pair("k_rsum", [P, C]), pair("att_s", [P, C * P])
        att_e = [pair(f"att_e{l}_", [P, C * (P + HC[l])]) for l in range(L)]
        y_rsum, y_n = pair("y_rsum", [P, T * 16]), pair("y_n", [P, N])
        y_stats, y_mv, y_rstd = pair("y_stats", [P, T * 6]), pair("y_mv", [P, T * 2]), pair("y_rstd", [P, T])
        y_nm, y_shift, y_z = pair("y_nm", [P, T]), pair("y_shift", [P, T]), pair("y_z", [P, N])
        icol = pair("icol", [P, 2 * C])
        h, th, g = pair("h", [P, N]), pair("th", [P, N]), pair("g", [P, N])
        g_hi, g_lo = pair("g_hi", [P, N], F16), pair("g_lo", [P, N], F16)

        ps_zk = bank("ps_zk")
        ps_qv = [bank(f"ps_qv{t}") for t in range(T)]
        ps_eo = bank("ps_eo")
        ps_qy = bank("ps_qy")
        ps_att = bank("ps_att")
        ps_y = [bank(f"ps_y{t}") for t in range(T)]

        const_in, cond_in, col_in, mask_in = map(sem, ("const_in", "cond_in", "col_in", "mask_in"))
        w_in_s = [sem(f"w_in{l}") for l in range(L)]
        w_late_in = [sem(f"w_late_in{l}") for l in range(L)]
        x_in = [sem(f"x_in{i}") for i in range(2)]
        m_row_in = [sem(f"m_row_in{i}") for i in range(2)]
        mask_rows_made, mask_rows_out = sem("mask_rows_made"), sem("mask_rows_out")
        ln_b_ready, w_scaled, w_hi_made, w_ready = map(sem, ("ln_b_ready", "w_scaled", "w_hi_made", "w_ready"))
        wo_scaled, wo_hi_made, wo_ready = map(sem, ("wo_scaled", "wo_hi_made", "wo_ready"))
        rows_done, rows_made, rows_scaled, rows_split = map(sem, ("rows_done", "rows_made", "rows_scaled", "rows_split"))
        rows_ready, ck_done, ck_made, ck_ready = map(sem, ("rows_ready", "ck_done", "ck_made", "ck_ready"))
        film_done, film_made, film_mixed, item_col_ready = map(
            sem, ("film_done", "film_made", "film_mixed", "item_col_ready"))
        cond_tanh, cond_silu, vmask_made = map(sem, ("cond_tanh", "cond_silu", "vmask_made"))
        neg_half_made, sel_cleared, sel_made, ind_made, block_mask_made = map(
            sem, ("neg_half_made", "sel_cleared", "sel_made", "ind_made", "block_mask_made"))
        x_bn, x_stats_ready, x_powered, x_shift_ready, z_ready = map(
            sem, ("x_bn", "x_stats_ready", "x_powered", "x_shift_ready", "z_ready"))
        zt_done, z_hi_ready, z_lo_ready = map(sem, ("zt_done", "z_hi_ready", "z_lo_ready"))
        k_done, k_add_ready, k_neg_ready, ek_ready = map(sem, ("k_done", "k_add_ready", "k_neg_ready", "ek_ready"))
        qv_done = [sem(f"qv{t}_done") for t in range(T)]
        q_max_ready, q_sub_ready, v_ready, eq_ready = map(sem, ("q_max_ready", "q_sub_ready", "v_ready", "eq_ready"))
        turned_done, ek_row_ready, eq_t_ready = map(sem, ("turned_done", "ek_row_ready", "eq_t_ready"))
        k_rsum_ready, att_done, att_s_ready, att_t_done, att_t_ready = map(
            sem, ("k_rsum_ready", "att_done", "att_s_ready", "att_t_done", "att_t_ready"))
        y_done, y_rsum_ready, y_n_ready, y_bn, y_stats_ready = map(
            sem, ("y_done", "y_rsum_ready", "y_n_ready", "y_bn", "y_stats_ready"))
        y_powered, y_shift_ready, y_z_ready, yzt_done = map(
            sem, ("y_powered", "y_shift_ready", "y_z_ready", "yzt_done"))
        vcol_ready, icol_ready, h_ready, th_ready, g_ready, g_hi_ready, g_lo_ready = map(
            sem, ("vcol_ready", "icol_ready", "h_ready", "th_ready", "g_ready", "g_hi_ready", "g_lo_ready"))
        o_done, x_new, out_out = map(sem, ("o_done", "x_new", "out_out"))

        block = ctx.enter_context(nc.Block())

        def wait_apart(engine, item, *waits):
            if not item.static:
                for _, value in waits:
                    engine.compute_val(value)
                engine.wait_ge(waits[0][0], 1)
            for semaphore, value in waits:
                engine.wait_ge(semaphore, value)

        def steps(engine, run):
            for front in range(0, 6):
                run(Step(0, front))
            with engine.Fori(6, B - 1, 2) as r:
                for u in range(2):
                    run(Step(r, u, 0))
            for front in range(B, B + 6):
                run(Step(0, front))
            with engine.Fori(B + 6, LAST - 1, 2) as r:
                for u in range(2):
                    run(Step(r, u, 1))
            for front in range(LAST, LAST + 4):
                run(Step(0, front))

        def at(step, back):
            return Item(step, back, B, L)

        def part(tile, i, width=D):
            return tile[:, i * width:(i + 1) * width]

        @block.sync
        def _(sp):
            sp.dma_start(col[:, :], columns).then_inc(col_in, 16)
            sp.dma_start(w_raw[0][:, :].rearrange("p (c n) -> p c n", c=C),
                         w_in[0].rearrange("(c p) n -> p c n", p=P)).then_inc(w_in_s[0], 16)
            sp.dma_start(m0r[:, :], mask0_row).then_inc(mask_in, 16)
            sp.dma_start(m1r[:, :], mask1_row).then_inc(mask_in, 16)
            sp.dma_start(row_b[0][:, :], rows[0].partition_broadcast(P)).then_inc(w_in_s[0], 16)
            sp.wait_ge(mask_rows_made, L)
            for l in range(L):
                sp.dma_start(mask_dram[l], m_add[l][:, :]).then_inc(mask_rows_out, 16)
            sp.wait_ge(mask_rows_out, 16 * L)

            def step(s):
                m, done = at(s, 1), at(s, 4)
                if m.exists:
                    j, p = m.index, m.parity
                    if not m.first_two:
                        sp.wait_ge(k_add_ready, j - 1)
                    row = mask_dram[m.layer, m.sequence] if m.static else mask_dram[m.layer, bass.ds(m.sequence, 1), :].rearrange("a n -> (a n)")
                    sp.dma_start(m_row[p][:, :], row.partition_broadcast(P)).then_inc(m_row_in[p], 16)
                if s.static and s.front == 2:
                    with sp.Fori(2, B - 1, 2) as b:
                        for u in range(2):
                            sp.wait_ge(x_in[u], 8 * b)
                            sp.dma_start(x_all[:, bass.ds((b + u) * N, N)].rearrange("p (a t f) -> p a t f", a=1, t=T),
                                         x_dram[:, bass.ds(b + u, 1)]).then_inc(x_in[u], 16)
                if done.exists and done.layer == 1:
                    sp.wait_ge(x_new, done.index + 1)
                    sp.dma_start(out_dram[:, bass.ds(done.sequence, 1)],
                                 x_all[:, bass.ds(done.sequence * N, N)].rearrange("p (a t f) -> p a t f", a=1, t=T))\
                      .then_inc(out_out, 16)

            steps(sp, step)
            sp.wait_ge(out_out, 16 * B)

        @block.scalar
        def _(act):
            act.dma_start(x_all[:, 0:N].rearrange("p (t f) -> p t f", t=T), x_dram[:, 0]).then_inc(x_in[0], 16)
            act.dma_start(ident[:, :], identity).then_inc(const_in, 16)
            act.dma_start(head_ind[:, :], indicators).then_inc(const_in, 16)
            act.dma_start(x_all[:, N:2 * N].rearrange("p (t f) -> p t f", t=T), x_dram[:, 1]).then_inc(x_in[1], 16)
            act.dma_start(cond[:, :], cond_t).then_inc(cond_in, 16)
            act.dma_start(m0c[:, :], mask0_col).then_inc(cond_in, 16)
            act.dma_start(m1c[:, :], mask1_col).then_inc(cond_in, 16)
            for l in range(L):
                if l:
                    act.dma_start(w_raw[l][:, :].rearrange("p (c n) -> p c n", c=C),
                                  w_in[l].rearrange("(c p) n -> p c n", p=P)).then_inc(w_in_s[l], 16)
                    act.dma_start(row_b[l][:, :], rows[l].partition_broadcast(P)).then_inc(w_in_s[l], 16)
                act.dma_start(wo_raw[l][:, :].rearrange("p (c n) -> p c n", c=C),
                              w_out[l].rearrange("(c p) n -> p c n", p=P)).then_inc(w_late_in[l], 16)
                act.dma_start(wemb[l][:, :].rearrange("p (c n) -> p c n", c=EC),
                              w_emb[l].rearrange("(c p) n -> p c n", p=P)).then_inc(w_late_in[l], 16)
            act.wait_ge(cond_in, 48)
            nc.scalar.activation(cond_t2[:, :], cond[:, :], ACT.Tanh, scale=0.5).then_inc(cond_tanh, 1)

            def z_high(a):
                j, p = a.index, a.parity
                act.wait_ge(zt_done, j + 1)
                if not a.first_two:
                    act.wait_ge(qv_done[T - 1], j - 1)
                nc.scalar.activation(z_hi[p][:, :], ps_zk[:, :], ACT.Copy, scale=Z_SCALE).then_inc(z_hi_ready, 1)

            def exps_turned(a):
                j, p = a.index, a.parity
                act.wait_ge(turned_done, j + 1)
                if not a.first_two:
                    act.wait_ge(y_done, j - 1)
                nc.scalar.activation(ek_row[p][:, :], ps_eo[:, :], ACT.Copy).then_inc(ek_row_ready, 1)
                nc.scalar.activation(eq_t[p][:, :], ps_qy[:, :], ACT.Copy).then_inc(eq_t_ready, 1)

            def exp_k(a):
                j, p = a.index, a.parity
                act.wait_ge(k_neg_ready, j + 1)
                if not a.first_two:
                    act.wait_ge(turned_done, j - 1)
                    act.wait_ge(k_rsum_ready, j - 1)
                for c in range(C):
                    last = nc.scalar.activation(part(ek[p], c), part(k_neg[p], c), ACT.Exp, scale=-1.0,
                                                bias=k_neg_max[p][:, c:c + 1], accum_out=k_sum[p][:, c:c + 1])
                last.then_inc(ek_ready, 1)

            def exp_q(a):
                j, p = a.index, a.parity
                act.wait_ge(q_sub_ready, T * j + T)
                if not a.first_two:
                    act.wait_ge(turned_done, j - 1)
                nc.scalar.activation(eq[p][:, :], q_sub[p][:, :], ACT.Exp, scale=1.0 / QKV_SCALE).then_inc(eq_ready, 1)

            def condition(a):
                j, p = a.index, a.parity
                act.wait_ge(yzt_done, j + 1)
                act.wait_ge(icol_ready, j + 1)
                if not a.first_two:
                    act.wait_ge(g_ready, j - 1)
                for c in range(C):
                    last = nc.scalar.activation(part(h[p], c), part(ps_qy, c), ACT.Identity,
                                                scale=icol[p][:, 2 * c:2 * c + 1], bias=icol[p][:, 2 * c + 1:2 * c + 2])
                last.then_inc(h_ready, 1)
                act.wait_ge(h_ready, j + 1)
                nc.scalar.activation(th[p][:, :], h[p][:, :], ACT.Tanh, scale=0.5).then_inc(th_ready, 1)

            def g_high(a):
                j, p = a.index, a.parity
                act.wait_ge(g_ready, j + 1)
                if not a.first_two:
                    act.wait_ge(o_done, j - 1)
                nc.scalar.activation(g_hi[p][:, :], g[p][:, :], ACT.Copy, scale=G_SCALE).then_inc(g_hi_ready, 1)

            def att_turned(a):
                j, p = a.index, a.parity
                act.wait_ge(att_t_done, j - B + 1)
                dst = att_e[1][p][:, :].rearrange("p (c n) -> p c n", c=C)[:, :, 0:P]
                nc.scalar.activation(dst, ps_att[:, C * P:2 * C * P].rearrange("p (c n) -> p c n", c=C), ACT.Copy)\
                  .then_inc(att_t_ready, 1)

            def normalise(a):
                j, p = a.index, a.parity
                act.wait_ge(x_shift_ready, j + 1)
                if not a.first_two:
                    act.wait_ge(zt_done, j - 1)
                for t in range(T):
                    last = nc.scalar.activation(part(z[p], t), x_all[:, bass.ds(a.sequence * N + t * D, D)], ACT.Identity,
                                                scale=x_rstd[p][:, t:t + 1], bias=x_shift[p][:, t:t + 1])
                last.then_inc(z_ready, 1)

            def v_masked(a, t):
                j, p = a.index, a.parity
                act.wait_ge(q_sub_ready, T * j + t + 1)
                if t == 0:
                    act.wait_ge(vcol_ready, j + 1)
                    if not a.first_two:
                        act.wait_ge(att_done, j - 1)
                nc.scalar.activation(part(v[p], t), ps_qv[t][:, D:2 * D], ACT.Copy, scale=vcol[p][:, t:t + 1])\
                  .then_inc(v_ready, 1)

            def step(s):
                tz, pr, aa, o = at(s, 1), at(s, 2), at(s, 3), at(s, 4)
                if tz.exists:
                    normalise(tz)
                if aa.exists:
                    exps_turned(aa)
                if pr.exists:
                    exp_k(pr)
                if o.exists:
                    condition(o)
                if pr.exists:
                    v_masked(pr, 0)
                if aa.exists and aa.layer == 1:
                    att_turned(aa)
                if o.exists:
                    g_high(o)
                if tz.exists:
                    z_high(tz)
                if pr.exists:
                    exp_q(pr)
                    v_masked(pr, 1)

            steps(act, step)

        @block.gpsimd
        def _(pool):
            pool.wait_ge(neg_half_made, 1)

            def indicators_in_place():
                pool.wait_ge(const_in, 32)
                first = 0
                for l in range(L):
                    for p in range(2):
                        for c in range(C):
                            base = c * (P + HC[l]) + P
                            last = pool.tensor_copy(att_e[l][p][:, base:base + HC[l]], head_ind[:, first:first + HC[l]])
                    first += HC[l]
                last.then_inc(ind_made, 1)

            def scale_and_shift(a, mv, ve, nm, rstd, shift, powered, done):
                j, p = a.index, a.parity
                pool.tensor_scalar(ve[p][:, :], mv[p][:, 1:2 * T:2], EPS, 1.0, ALU.add, ALU.mult)
                pool.tensor_scalar(nm[p][:, :], mv[p][:, 0:2 * T:2], -1.0, 0.0, ALU.mult, ALU.add).then_inc(powered, 1)
                pool.wait_ge(powered, 2 * j + 1)
                pool.tensor_tensor(rstd[p][:, :], ve[p][:, :], neg_half[:, :], ALU.pow).then_inc(powered, 1)
                pool.wait_ge(powered, 2 * j + 2)
                pool.tensor_tensor(shift[p][:, :], nm[p][:, :], rstd[p][:, :], ALU.mult).then_inc(done, 1)

            def x_scale(a):
                j, p = a.index, a.parity
                free = [] if a.first_two else [(z_ready, j - 1)]
                wait_apart(pool, a, (x_stats_ready, j + 1), *free)
                scale_and_shift(a, x_mv, x_ve, x_nm, x_rstd, x_shift, x_powered, x_shift_ready)

            def k_addend(a):
                j, p = a.index, a.parity
                if a.starts_layer:
                    pool.wait_ge(ck_ready, a.layer + 1)
                free = [] if a.first_two else [(k_neg_ready, j - 1)]
                wait_apart(pool, a, (m_row_in[p], 8 * (j - p) + 16), *free)
                for c in range(C):
                    last = pool.tensor_scalar(part(k_add[p], c), m_row[p][:, :], ck[a.layer][:, c:c + 1], 1.0,
                                              ALU.add, ALU.mult)
                last.then_inc(k_add_ready, 1)

            def v_columns(a):
                j, p = a.index, a.parity
                if a.starts_layer and a.layer == 0:
                    pool.wait_ge(vmask_made, 1)
                if not a.first_two:
                    pool.wait_ge(v_ready, T * (j - 1))
                first = a.sequence * 6 + 2 * C
                pool.tensor_copy(vcol[p][:, :], item_col[a.layer][:, bass.ds(first, T)]).then_inc(vcol_ready, 1)

            def ab_columns(a):
                j, p = a.index, a.parity
                if a.starts_layer:
                    pool.wait_ge(item_col_ready, a.layer + 1)
                if not a.first_two:
                    pool.wait_ge(h_ready, j - 1)
                pool.tensor_copy(icol[p][:, :], item_col[a.layer][:, bass.ds(a.sequence * 6, 2 * C)])\
                    .then_inc(icol_ready, 1)

            def y_normalise(a):
                j, p = a.index, a.parity
                free = [] if a.first_two else [(yzt_done, j - 1)]
                wait_apart(pool, a, (y_stats_ready, j + 1), *free)
                scale_and_shift(a, y_mv, y_ve, y_nm, y_rstd, y_shift, y_powered, y_shift_ready)
                wait_apart(pool, a, (y_shift_ready, j + 1))
                for t in range(T):
                    last = pool.tensor_scalar(part(y_z[p], t), part(y_n[p], t), y_rstd[p][:, t:t + 1],
                                              y_shift[p][:, t:t + 1], ALU.mult, ALU.add)
                last.then_inc(y_z_ready, 1)

            def step(s):
                f, m, o = at(s, 0), at(s, 1), at(s, 4)
                if o.exists:
                    y_normalise(o)
                    ab_columns(o)
                if f.exists:
                    x_scale(f)
                if m.exists:
                    k_addend(m)
                    v_columns(m)
                if s.static and s.front == 1:
                    indicators_in_place()

            steps(pool, step)

        @block.vector
        def _(dve):
            vec = nc.vector

            def constants():
                vec.memset(neg_half[:, :], -0.5).then_inc(neg_half_made, 1)
                vec.memset(sel_q[:, :], 0.0)
                vec.memset(sel_o[:, :], 0.0).then_inc(sel_cleared, 1)
                dve.wait_ge(sel_cleared, 1)
                for r in (0, 32):
                    vec.memset(sel_q[r:r + 1, :], Z_SCALE)
                    last = vec.memset(sel_o[r:r + 1, :], 2.0 * G_SCALE)
                last.then_inc(sel_made, 1)

            def mask_rows():
                dve.wait_ge(mask_in, 32)
                vec.tensor_scalar(m_add[0][:, :], m0r[:, :], -1.0, MASK0 * QKV_SCALE, ALU.add, ALU.mult)\
                   .then_inc(mask_rows_made, 1)
                vec.tensor_scalar(m_add[1][:, :], m1r[:, :], 1.0, -MASK1, ALU.is_equal, ALU.mult)\
                   .then_inc(mask_rows_made, 1)

            def block_masks():
                dve.wait_ge(const_in, 32)
                first = 0
                for l in range(L):
                    last = vec.tensor_copy(block_mask[l][:, :].rearrange("p (h d) -> p h d", d=DH[l]),
                                           head_ind[:, first:first + HC[l]].unsqueeze(2).to_broadcast([P, HC[l], DH[l]]))
                    first += HC[l]
                last.then_inc(block_mask_made, 1)

            def value_masks():
                dve.wait_ge(cond_in, 48)
                for t in range(T):
                    it = [item_col[l][:, :].rearrange("p (b k) -> p k b", k=6)[:, 2 * C + t, :] for l in range(L)]
                    vec.tensor_scalar(it[0], m0c[:, t * B:(t + 1) * B], 1.0 / QKV_SCALE, None, ALU.mult)
                    last = vec.tensor_scalar(it[1], m1c[:, t * B:(t + 1) * B], 1.0, 1.0 / QKV_SCALE,
                                             ALU.not_equal, ALU.mult)
                last.then_inc(vmask_made, 1)

            def ln_bias(l):
                dve.wait_ge(col_in, 16)
                for c in range(C):
                    b = col[:, 18 * l + 2 + c:18 * l + 3 + c]
                    last = vec.tensor_copy(ln_b[l][:, c * P:(c + 1) * P], b.to_broadcast([P, P]))
                last.then_inc(ln_b_ready, 1)

            def layer_weights(l):
                dve.wait_ge(w_in_s[l], 32)
                if l:
                    dve.wait_ge(wo_ready, l)
                W = 3 * D
                for c in range(C):
                    last = vec.tensor_scalar(w_tmp[:, c * W:(c + 1) * W], w_raw[l][:, c * W:(c + 1) * W],
                                             col[:, 18 * l + c:18 * l + c + 1], W_SCALE, ALU.mult, ALU.mult)
                last.then_inc(w_scaled, 1)
                dve.wait_ge(w_scaled, l + 1)
                vec.tensor_copy(w_hi[l][:, :], w_tmp[:, :]).then_inc(w_hi_made, 1)
                dve.wait_ge(w_hi_made, l + 1)
                vec.tensor_tensor(w_lo[l][:, :], w_tmp[:, :], w_hi[l][:, :], ALU.subtract).then_inc(w_ready, 1)

            def out_weights(l):
                dve.wait_ge(w_late_in[l], 32)
                dve.wait_ge(w_ready, l + 1)
                vec.tensor_scalar(w_tmp[:, 0:C * D], wo_raw[l][:, :], W_SCALE, None, ALU.mult).then_inc(wo_scaled, 1)
                dve.wait_ge(wo_scaled, l + 1)
                vec.tensor_copy(wo_hi[l][:, :], w_tmp[:, 0:C * D]).then_inc(wo_hi_made, 1)
                dve.wait_ge(wo_hi_made, l + 1)
                vec.tensor_tensor(wo_lo[l][:, :], w_tmp[:, 0:C * D], wo_hi[l][:, :], ALU.subtract).then_inc(wo_ready, 1)

            def k_bias(l, bank):
                dve.wait_ge(ck_done, l + 1)
                vec.tensor_tensor(ck[l][:, :], bank[:, 0:C], col[:, 18 * l + 4:18 * l + 6], ALU.add).then_inc(ck_made, 1)
                dve.wait_ge(ck_made, l + 1)
                vec.tensor_scalar(ck[l][:, :], ck[l][:, :], QKV_SCALE, None, ALU.mult).then_inc(ck_ready, 1)

            def row_biases(l, bank):
                dve.wait_ge(rows_done, l + 1)
                if l:
                    dve.wait_ge(rows_ready, l)
                vec.tensor_tensor(bias_row[:, 0:2 * D], bank[0:64, :], row_b[l][0:64, 0:2 * D], ALU.add)
                vec.tensor_copy(bias_row[:, 2 * D:3 * D], row_b[l][0:64, bo:bo + D]).then_inc(rows_made, 1)
                dve.wait_ge(rows_made, l + 1)
                vec.tensor_scalar(bias_tmp[:, :], bias_row[:, :], W_SCALE, None, ALU.mult).then_inc(rows_scaled, 1)
                dve.wait_ge(rows_scaled, l + 1)
                vec.tensor_copy(bias_hi_lo[l][:, :], bias_tmp[:, :]).then_inc(rows_split, 1)
                dve.wait_ge(rows_split, l + 1)
                vec.tensor_tensor(bias_hi_lo[l][32:64, :], bias_tmp[32:64, :], bias_hi_lo[l][32:64, :],
                                  ALU.subtract).then_inc(rows_ready, 1)

            def silu_cond():
                dve.wait_ge(cond_tanh, 1)
                vec.scalar_tensor_tensor(cond_s[:, :], cond_t2[:, :], 1.0, cond[:, :], ALU.add, ALU.mult)\
                   .then_inc(cond_silu, 1)

            def film_columns(l, bank, first):
                base = 18 * l
                dve.wait_ge(film_done, l + 1)
                if l:
                    dve.wait_ge(item_col_ready, l)
                for e in range(2 * C):
                    last = vec.tensor_scalar(film[:, e * B:(e + 1) * B], bank[:, first + e * B:first + (e + 1) * B], 0.5,
                                             col[:, base + 6 + e:base + 7 + e], ALU.mult, ALU.add)
                last.then_inc(film_made, 1)
                dve.wait_ge(film_made, l + 1)
                it = item_col[l][:, :].rearrange("p (b k) -> p k b", k=6)
                for c in range(C):
                    l2w, l2b = col[:, base + 10 + c:base + 11 + c], col[:, base + 12 + c:base + 13 + c]
                    vec.tensor_scalar(it[:, 2 * c, :], film[:, c * B:(c + 1) * B], 1.0, l2w, ALU.add, ALU.mult)
                    last = vec.tensor_scalar(it[:, 2 * c + 1, :], film[:, c * B:(c + 1) * B], 1.0, l2b, ALU.add, ALU.mult)
                last.then_inc(film_mixed, 1)
                dve.wait_ge(film_mixed, l + 1)
                for c in range(C):
                    last = vec.tensor_tensor(it[:, 2 * c + 1, :], it[:, 2 * c + 1, :],
                                             film[:, (C + c) * B:(C + c + 1) * B], ALU.add)
                last.then_inc(item_col_ready, 1)

            def x_statistics(a):
                j, p = a.index, a.parity
                if a.layer == 0:
                    dve.wait_ge(x_in[p], 8 * (j - p) + 16)
                else:
                    dve.wait_ge(x_new, j - B + 1)
                for t in range(T):
                    last = vec.bn_stats(x_stats[p][:, 6 * t:6 * t + 6], x_all[:, bass.ds(a.sequence * N + t * D, D)])
                last.then_inc(x_bn, 1)

            def x_aggregate(a):
                j, p = a.index, a.parity
                free = [] if a.first_two else [(x_shift_ready, j - 1)]
                wait_apart(dve, a, (x_bn, j + 1), *free)
                for t in range(T):
                    last = vec.bn_aggr(x_mv[p][:, 2 * t:2 * t + 2], x_stats[p][:, 6 * t:6 * t + 6])
                last.then_inc(x_stats_ready, 1)

            def z_low(a):
                j, p = a.index, a.parity
                dve.wait_ge(z_hi_ready, j + 1)
                vec.scalar_tensor_tensor(z_lo[p][:, :], ps_zk[:, :], Z_SCALE, z_hi[p][:, :], ALU.mult, ALU.subtract)\
                   .then_inc(z_lo_ready, 1)

            def k_shift(a):
                j, p = a.index, a.parity
                free = [] if a.first_two else [(ek_ready, j - 1)]
                wait_apart(dve, a, (k_done, j + 1), (k_add_ready, j + 1), *free)
                for c in range(C):
                    last = vec.tensor_tensor_reduce(out=part(k_neg[p], c), in0=part(ps_zk, c), in1=part(k_add[p], c),
                                                    scale=-1.0 / QKV_SCALE, scalar=BIG, op0=ALU.add, op1=ALU.min,
                                                    accum_out=k_neg_max[p][:, c:c + 1])
                last.then_inc(k_neg_ready, 1)

            def q_maximum(a, t):
                j, p, l = a.index, a.parity, a.layer
                dve.wait_ge(qv_done[t], j + 1)
                q = ps_qv[t][:, 0:D].rearrange("p (h d) -> p h d", d=DH[l])
                vec.tensor_reduce(q_max[p][:, t * 16:t * 16 + HEADS[l]], q, AX_X, ALU.max).then_inc(q_max_ready, 1)

            def q_shift(a, t):
                j, p, l = a.index, a.parity, a.layer
                dve.wait_ge(q_max_ready, T * j + t + 1)
                if t == 0 and not a.first_two:
                    dve.wait_ge(eq_ready, j - 1)
                q = ps_qv[t][:, 0:D].rearrange("p (h d) -> p h d", d=DH[l])
                q_m = q_max[p][:, t * 16:t * 16 + HEADS[l]]
                vec.tensor_tensor(part(q_sub[p], t).rearrange("p (h d) -> p h d", d=DH[l]), q,
                                  q_m.unsqueeze(2).to_broadcast([P, HEADS[l], DH[l]]), ALU.subtract)\
                   .then_inc(q_sub_ready, 1)

            def k_sums(a):
                j, p = a.index, a.parity
                dve.wait_ge(ek_ready, j + 1)
                vec.reciprocal(k_rsum[p][:, :], k_sum[p][:, :]).then_inc(k_rsum_ready, 1)

            def att_scale(a):
                j, p, l = a.index, a.parity, a.layer
                dve.wait_ge(k_rsum_ready, j + 1)
                dve.wait_ge(att_done, j + 1)
                if not a.first_two:
                    dve.wait_ge(y_done, j - 1)
                for c in range(C):
                    base = c * (P + HC[l])
                    dst = att_e[l][p][:, base:base + P] if l == 0 else part(att_s[p], c, P)
                    last = vec.scalar_tensor_tensor(dst, part(ps_att, c, P), k_rsum[p][:, c:c + 1],
                                                    block_mask[l][:, :], ALU.mult, ALU.mult)
                last.then_inc(att_s_ready, 1)

            def y_views(a):
                W = P + HC[a.layer]
                y = [ps_y[t][:, 0:C * W].rearrange("p (c n) -> p c n", c=C) for t in range(T)]
                r = [y_rsum[a.parity][:, t * 16:t * 16 + HEADS[a.layer]].rearrange("p (c n) -> p c n", c=C)
                     for t in range(T)]
                return [v[:, :, 0:P] for v in y], [v[:, :, P:W] for v in y], r

            def y_sums(a):
                dve.wait_ge(y_done, a.index + 1)
                _, sums, r = y_views(a)
                for t in range(T):
                    last = vec.reciprocal(r[t], sums[t])
                last.then_inc(y_rsum_ready, 1)

            def y_divide(a):
                j, p, l = a.index, a.parity, a.layer
                y, _, r = y_views(a)
                dve.wait_ge(y_rsum_ready, j + 1)
                if not a.first_two:
                    dve.wait_ge(y_z_ready, j - 1)
                for t in range(T):
                    last = vec.tensor_tensor(part(y_n[p], t).rearrange("p (c h d) -> p c h d", c=C, d=DH[l]),
                                             y[t].rearrange("p c (h d) -> p c h d", d=DH[l]),
                                             r[t].unsqueeze(3).to_broadcast([P, C, HC[l], DH[l]]), ALU.mult)
                last.then_inc(y_n_ready, 1)

            def y_statistics(a):
                j, p = a.index, a.parity
                dve.wait_ge(y_n_ready, j + 1)
                for t in range(T):
                    last = vec.bn_stats(y_stats[p][:, 6 * t:6 * t + 6], part(y_n[p], t))
                last.then_inc(y_bn, 1)

            def y_aggregate(a):
                j, p = a.index, a.parity
                wait_apart(dve, a, (y_bn, j + 1))
                for t in range(T):
                    last = vec.bn_aggr(y_mv[p][:, 2 * t:2 * t + 2], y_stats[p][:, 6 * t:6 * t + 6])
                last.then_inc(y_stats_ready, 1)

            def gate(a):
                j, p = a.index, a.parity
                dve.wait_ge(th_ready, j + 1)
                vec.scalar_tensor_tensor(g[p][:, :], th[p][:, :], 1.0, h[p][:, :], ALU.add, ALU.mult).then_inc(g_ready, 1)

            def g_low(a):
                j, p = a.index, a.parity
                dve.wait_ge(g_hi_ready, j + 1)
                vec.scalar_tensor_tensor(g_lo[p][:, :], g[p][:, :], G_SCALE, g_hi[p][:, :], ALU.mult, ALU.subtract)\
                   .then_inc(g_lo_ready, 1)

            def residual(a):
                j = a.index
                dve.wait_ge(o_done, j + 1)
                xs = x_all[:, bass.ds(a.sequence * N, N)]
                vec.scalar_tensor_tensor(xs, ps_eo[:, :], 1.0 / OUT_SCALE, xs, ALU.mult, ALU.add).then_inc(x_new, 1)

            constants()
            ln_bias(0)
            mask_rows()
            layer_weights(0)

            def step(s):
                f, tz, pr, aa, o = (at(s, back) for back in range(5))
                if pr.exists:
                    k_shift(pr)
                if f.exists:
                    x_statistics(f)
                if aa.exists:
                    k_sums(aa)
                if f.exists:
                    x_aggregate(f)
                if s.static and s.front == 0:
                    k_bias(0, ps_y[0])
                    row_biases(0, ps_att)
                    block_masks()
                    value_masks()
                if pr.exists:
                    q_maximum(pr, 0)
                    q_shift(pr, 0)
                if aa.exists:
                    att_scale(aa)
                if o.exists:
                    gate(o)
                if pr.exists:
                    q_maximum(pr, 1)
                if o.exists:
                    g_low(o)
                if aa.exists:
                    y_sums(aa)
                if pr.exists:
                    q_shift(pr, 1)
                if aa.exists:
                    y_divide(aa)
                if tz.exists:
                    z_low(tz)
                if aa.exists:
                    y_statistics(aa)
                if o.exists:
                    residual(o)
                if aa.exists:
                    y_aggregate(aa)
                if s.static and s.front == 2:
                    silu_cond()
                    out_weights(0)
                    film_columns(0, ps_y[0], 0)
                    layer_weights(1)
                    ln_bias(1)
                if s.static and s.front == 3:
                    row_biases(1, ps_att)
                if s.static and s.front == 4:
                    k_bias(1, ps_att)
                    film_columns(1, ps_att, 64)
                    out_weights(1)

            steps(dve, step)

        @block.tensor
        def _(pe):
            mm, turn = nc.tensor.matmul, nc.tensor.transpose
            W = 3 * D

            def row_bias_products(l, bank):
                pe.wait_ge(w_in_s[l], 32)
                pe.wait_ge(ln_b_ready, l + 1)
                if l:
                    pe.wait_ge(att_s_ready, 1)
                for c in range(C):
                    last = mm(bank[:, :], ln_b[l][:, c * P:(c + 1) * P], w_raw[l][:, c * W + D:(c + 1) * W],
                              start=(c == 0), stop=(c == C - 1))
                last.then_inc(rows_done, 1)

            def k_bias_products(l, bank):
                if l:
                    pe.wait_ge(rows_ready, l + 1)
                    pe.wait_ge(att_s_ready, 2)
                for d in range(C):
                    for c in range(C):
                        last = mm(bank[:, d:d + 1], w_raw[l][:, c * W + d * P:c * W + (d + 1) * P],
                                  ln_b[l][:, c * P:c * P + 1], start=(c == 0), stop=(c == C - 1))
                last.then_inc(ck_done, 1)

            def film_products(l, bank, first):
                pe.wait_ge(w_late_in[l], 32)
                pe.wait_ge(cond_silu, 1)
                pe.wait_ge(ck_made, l + 1)
                for e in range(2 * C):
                    for c in range(EC):
                        last = mm(bank[:, first + e * B:first + (e + 1) * B],
                                  wemb[l][:, c * 2 * D + e * P:c * 2 * D + (e + 1) * P],
                                  cond_s[:, c * B:(c + 1) * B], start=(c == 0), stop=(c == EC - 1))
                last.then_inc(film_done, 1)

            def turn_z(a):
                j, p = a.index, a.parity
                pe.wait_ge(z_ready, j + 1)
                if not (a.static and a.index == 0):
                    pe.wait_ge(k_neg_ready, j)
                for c in range(C):
                    for t in range(T):
                        last = turn(ps_zk[:, c * S + t * P:c * S + (t + 1) * P],
                                    z[p][:, t * D + c * P:t * D + (c + 1) * P], ident[:, :])
                last.then_inc(zt_done, 1)

            def project_k(a):
                j, p, l = a.index, a.parity, a.layer
                pe.wait_ge(z_lo_ready, j + 1)
                if a.starts_layer:
                    pe.wait_ge(w_ready, l + 1)
                for d in range(C):
                    n = 0
                    for c in range(C):
                        for w, zz in ((w_hi, z_hi), (w_hi, z_lo), (w_lo, z_hi)):
                            last = mm(part(ps_zk, d), w[l][:, c * W + d * P:c * W + (d + 1) * P], part(zz[p], c),
                                      start=(n == 0), stop=(n == 3 * C - 1))
                            n += 1
                last.then_inc(k_done, 1)

            def project_qv(a, t, between=None):
                j, p, l = a.index, a.parity, a.layer
                if a.starts_layer and t == 0:
                    pe.wait_ge(rows_ready, l + 1)
                    pe.wait_ge(sel_made, 1)
                if not (a.static and a.index == 0):
                    pe.wait_ge(v_ready, T * (j - 1) + t + 1)
                n = 0
                for c in range(C):
                    for zz, w in ((z_hi, w_hi), (z_hi, w_lo), (z_lo, w_hi)):
                        last = mm(ps_qv[t][:, :], zz[p][:, c * S + t * P:c * S + (t + 1) * P], w[l][:, c * W + D:(c + 1) * W],
                           start=(n == 0), stop=(n == 3 * C - 1))
                        if n == 0:
                            mm(ps_qv[t][:, :], sel_q[:, :], bias_hi_lo[l][:, 0:2 * D], start=False, stop=False)
                        n += 1
                    if c == 0 and between:
                        between()
                last.then_inc(qv_done[t], 1)

            def turn_exps(a):
                j, p = a.index, a.parity
                pe.wait_ge(ek_ready, j + 1)
                if not a.first_two:
                    pe.wait_ge(x_new, j - 1)
                for t in range(T):
                    for c in range(C):
                        turn(ps_eo[:, t * D + c * P:t * D + (c + 1) * P],
                             ek[p][:, c * S + t * P:c * S + (t + 1) * P], ident[:, :])
                pe.wait_ge(eq_ready, j + 1)
                if not a.first_two:
                    pe.wait_ge(h_ready, j - 1)
                for c in range(C):
                    for t in range(T):
                        last = turn(ps_qy[:, c * S + t * P:c * S + (t + 1) * P],
                                    eq[p][:, t * D + c * P:t * D + (c + 1) * P], ident[:, :])
                last.then_inc(turned_done, 1)

            def attend(a):
                j, p, l = a.index, a.parity, a.layer
                pe.wait_ge(ek_row_ready, j + 1)
                pe.wait_ge(v_ready, T * j + T)
                if a.static and a.index == 0:
                    pe.wait_ge(rows_ready, 1)
                elif a.static and a.index == 1:
                    pe.wait_ge(rows_ready, 2)
                elif a.static and a.index == 2:
                    pe.wait_ge(item_col_ready, 2)
                if not (a.static and a.index == 0):
                    if a.after_layer1:
                        pe.wait_ge(att_t_ready, j - B)
                    else:
                        pe.wait_ge(att_s_ready, j)
                for c in range(C):
                    for t in range(T):
                        last = mm(part(ps_att, c, P), ek_row[p][:, t * D + c * P:t * D + (c + 1) * P],
                                  v[p][:, t * D + c * P:t * D + (c + 1) * P], start=(t == 0), stop=(t == T - 1))
                last.then_inc(att_done, 1)

            def turn_att(a):
                j, p = a.index, a.parity
                pe.wait_ge(att_s_ready, j + 1)
                for c in range(C):
                    last = turn(part(ps_att, C + c, P), part(att_s[p], c, P), ident[:, :])
                last.then_inc(att_t_done, 1)

            def attention_out(a):
                j, p, l = a.index, a.parity, a.layer
                E = P + HC[l]
                pe.wait_ge(eq_t_ready, j + 1)
                if l == 0:
                    pe.wait_ge(att_s_ready, j + 1)
                else:
                    pe.wait_ge(att_t_ready, j - B + 1)
                if a.static and a.index == 0:
                    pe.wait_ge(ind_made, 1)
                    pe.wait_ge(film_made, 1)
                else:
                    pe.wait_ge(y_n_ready, j)
                for t in range(T):
                    for c in range(C):
                        last = mm(part(ps_y[t], c, E), eq_t[p][:, c * S + t * P:c * S + (t + 1) * P],
                                  part(att_e[l][p], c, E), start=True, stop=True)
                last.then_inc(y_done, 1)

            def turn_y(a):
                j, p = a.index, a.parity
                pe.wait_ge(y_z_ready, j + 1)
                if a.next_exists:
                    pe.wait_ge(eq_t_ready, j + 2)
                for c in range(C):
                    for t in range(T):
                        last = turn(ps_qy[:, c * S + t * P:c * S + (t + 1) * P],
                                    y_z[p][:, t * D + c * P:t * D + (c + 1) * P], ident[:, :])
                last.then_inc(yzt_done, 1)

            def project_out(a):
                j, p, l = a.index, a.parity, a.layer
                pe.wait_ge(g_lo_ready, j + 1)
                if a.starts_layer:
                    pe.wait_ge(wo_ready, l + 1)
                if a.next_exists:
                    pe.wait_ge(ek_row_ready, j + 2)
                for t in range(T):
                    n = 0
                    for c in range(C):
                        for gg, w in ((g_hi, wo_hi), (g_hi, wo_lo), (g_lo, wo_hi)):
                            mm(part(ps_eo, t), gg[p][:, c * S + t * P:c * S + (t + 1) * P], part(w[l], c),
                               start=(n == 0), stop=False)
                            n += 1
                    last = mm(part(ps_eo, t), sel_o[:, :], bias_hi_lo[l][:, 2 * D:3 * D], start=False, stop=True)
                last.then_inc(o_done, 1)

            row_bias_products(0, ps_att)
            k_bias_products(0, ps_y[0])
            pe.wait_ge(const_in, 32)

            def step(s):
                tz, pr, aa, o = (at(s, back) for back in range(1, 5))
                if pr.exists:
                    project_k(pr)
                if aa.exists:
                    turn_exps(aa)
                if pr.exists:
                    project_qv(pr, 0)
                if o.exists:
                    turn_y(o)
                if aa.exists:
                    attend(aa)
                turns = aa.exists and aa.layer == 1
                if pr.exists:
                    project_qv(pr, 1, (lambda: turn_att(aa)) if turns else None)
                elif turns:
                    turn_att(aa)
                if aa.exists:
                    attention_out(aa)
                if tz.exists:
                    turn_z(tz)
                if o.exists:
                    project_out(o)
                if s.static and s.front == 2:
                    film_products(0, ps_y[0], 0)
                if s.static and s.front == 3:
                    row_bias_products(1, ps_att)
                if s.static and s.front == 4:
                    k_bias_products(1, ps_att)
                    film_products(1, ps_att, 64)

            steps(pe, step)


def kernel(**inputs):
    import numpy as np
    import concourse.bacc as bacc
    from concourse.bass_utils import run_bass_kernel_spmd as run

    f = {n: np.asarray(a) for n, a in inputs.items()}
    P, B, S = 128, f["x"].shape[0], f["x"].shape[1]
    names = [dict(lw="L0_cond_ln_w", lb="L0_cond_ln_b", q="L0_cond_Wq", bq="L0_cond_bq", k="L0_cond_Wk", bk="L0_cond_bk",
                  v="L0_cond_Wv", bv="L0_cond_bv", e="L0_cond_W_emb", be="L0_cond_b_emb", l2w="L0_cond_ln2_w",
                  l2b="L0_cond_ln2_b", o="L0_cond_W_out", bo="L0_cond_b_out"),
             dict(lw="L1_cond_norm_scale", lb="L1_cond_norm_bias", q="L1_cond_Wq", bq="L1_cond_bq", k="L1_cond_Wk",
                  bk="L1_cond_bk", v="L1_cond_Wv", bv="L1_cond_bv", e="L1_cond_film_emb_W", be="L1_cond_film_emb_b",
                  l2w="L1_cond_film_norm_scale", l2b="L1_cond_film_norm_bias", o="L1_cond_film_out_W",
                  bo="L1_cond_film_out_b")]

    def column(a):
        return a.reshape(-1, P).T

    def head_indicators():
        return np.concatenate([np.arange(P)[:, None] // d == np.arange(P // d)[None, :] for d in (32, 16)], 1)

    arrays = {
        "x": f["x"],
        "cond_t": f["cond_2048"].T.reshape(-1, P, B).transpose(1, 0, 2).reshape(P, -1),
        "mask0_row": f["mask_BxSx1_fk1"].reshape(B, S),
        "mask1_row": f["mask_BxS_ik0"],
        "mask0_col": f["mask_BxSx1_fk1"].reshape(B, S // P, P).transpose(2, 1, 0).reshape(P, -1),
        "mask1_col": f["mask_BxS_ik0"].reshape(B, S // P, P).transpose(2, 1, 0).reshape(P, -1),
        "identity": np.eye(P, dtype=np.float32),
        "indicators": head_indicators().astype(np.float32),
        "columns": np.concatenate([np.concatenate([column(f[n[i]]) for i in ("lw", "lb", "bk", "be", "l2w", "l2b")]
                                                  + [np.zeros((P, 4), np.float32)], 1) for n in names], 1),
        "rows": np.stack([np.concatenate([f[n[i]] for i in ("bq", "bv", "bo")]) for n in names]),
        "w_in": np.stack([np.concatenate([f[n[i]] for i in ("k", "q", "v")], 1) for n in names]),
        "w_emb": np.stack([f[n["e"]] for n in names]),
        "w_out": np.stack([f[n["o"]] for n in names]),
    }
    arrays = {n: np.ascontiguousarray(a) for n, a in arrays.items()}
    nc = bacc.Bacc("TRN2", target_bir_lowering=False, num_devices=1)
    aps = {n: nc.dram_tensor(f"in_{n}", a.shape, mybir.dt.from_np(a.dtype), kind="ExternalInput").ap()
           for n, a in arrays.items()}
    out = nc.dram_tensor("out_0", f["x"].shape, F32, kind="ExternalOutput").ap()
    two_layers(nc, out=out, **aps)
    r = run(nc, [{f"in_{n}": a for n, a in arrays.items()}], core_ids=[0])
    return r.results[0]["out_0"]
```

```python
from contextlib import ExitStack

import concourse.bass as bass
from concourse import mybir

P = 128
ACT = mybir.ActivationFunctionType
ALU = mybir.AluOpType
F32 = mybir.dt.float32
F16 = mybir.dt.float16
I32 = mybir.dt.int32
AX_X = mybir.AxisListType.X

EPS = 1e-5
Z_SCALE = 256.0
W_SCALE = 64.0
G_SCALE = 64.0
QKV_SCALE = Z_SCALE * W_SCALE
OUT_SCALE = G_SCALE * W_SCALE * 2.0
MASK0 = 1.0e6
MASK1 = 1.0e30
BIG = 3.0e38
COLUMNS = 14


class Step:

    def __init__(self, base, front, layer=None):
        self.base, self.front, self.layer = base, front, layer
        self.static = layer is None


class Item:

    def __init__(self, step, back, sequences, layers):
        k = step.front - back
        self.index = step.base + k
        self.parity = k % 2
        self.static = step.static
        self.exists = not step.static or 0 <= k < sequences * layers
        self.layer = k // sequences if step.static else step.layer
        self.sequence = self.index - self.layer * sequences
        self.first_two = step.static and k < 2
        self.starts_layer = step.static and k % sequences == 0
        self.next_exists = not step.static or k < sequences * layers - 1


def two_layers(nc, x, cond_t, mask0_row, mask1_row, mask0_col, mask1_col, identity, indicators,
               columns, rows, w_in, w_emb, w_out, out):
    B, S, D = x.shape
    L = w_in.shape[0]
    TE = w_emb.shape[1]
    T, C, EC = S // P, D // P, TE // P
    DH = (32, 16)
    HEADS = [D // d for d in DH]
    HC = [P // d for d in DH]
    N = T * D
    LAST = B * L
    assert T == 2 and C == 2 and L == 2 and B % 2 == 0

    x_dram = x.rearrange("b (t p) f -> p b t f", p=P)
    out_dram = out.rearrange("b (t p) f -> p b t f", p=P)
    mask_dram = nc.dram_tensor("mask_rows", (L, B, S), F32, kind="Internal").ap()

    ctx = ExitStack()
    with ctx:
        def sb(name, shape, dt=F32):
            return ctx.enter_context(nc.sbuf_tensor(name, shape, dt))

        def pair(name, shape, dt=F32):
            return [sb(f"{name}{i}", shape, dt) for i in range(2)]

        def bank(name):
            return ctx.enter_context(nc.psum_tensor(name, [P, 512], F32))

        def sem(name):
            return ctx.enter_context(nc.semaphore(name))

        x_all = sb("x_all", [P, B * N])
        ident = sb("ident", [P, P])
        head_ind = sb("head_ind", [P, sum(HC)])
        block_mask = [sb(f"block_mask{l}", [P, P]) for l in range(L)]
        col = sb("col", [P, L * COLUMNS])
        w_raw = [sb(f"w_raw{l}", [P, C * 3 * D]) for l in range(L)]
        wo_raw = [sb(f"wo_raw{l}", [P, C * D]) for l in range(L)]
        bo = 2 * D
        wemb = [sb(f"wemb{l}", [P, EC * 2 * D]) for l in range(L)]
        row_b = [sb(f"row_b{l}", [P, 3 * D]) for l in range(L)]
        w_hi = [sb(f"w_hi{l}", [P, C * 3 * D], F16) for l in range(L)]
        w_lo = [sb(f"w_lo{l}", [P, C * 3 * D], F16) for l in range(L)]
        lnw = [sb(f"lnw{l}", [P, C]) for l in range(L)]
        wo_hi = [sb(f"wo_hi{l}", [P, C * D], F16) for l in range(L)]
        wo_lo = [sb(f"wo_lo{l}", [P, C * D], F16) for l in range(L)]
        ln_b = [sb(f"ln_b{l}", [P, C * P]) for l in range(L)]
        ck = [sb(f"ck{l}", [P, C]) for l in range(L)]
        bias_hi_lo = [sb(f"bias_hi_lo{l}", [P, 2 * D], F16) for l in range(L)]
        bias_row = sb("bias_row", [64, 2 * D])
        sel_q = sb("sel_q", [P, P], F16)
        cond = sb("cond", [P, EC * B])
        cond_s = sb("cond_s", [P, EC * B])
        cond_t2 = sb("cond_t2", [P, EC * B])
        film = sb("film", [P, 4 * B])
        item_col = [sb(f"item_col{l}", [P, B * 6]) for l in range(L)]
        m0c = sb("m0c", [P, B * T])
        m1c = sb("m1c", [P, B * T], I32)
        m0r = sb("m0r", [B, S])
        m1r = sb("m1r", [B, S], I32)
        m_add = [sb(f"m_add{l}", [B, S]) for l in range(L)]
        neg_half = sb("neg_half", [P, T])
        act_first = sb("act_first", [P, T])

        x_stats, x_mv, x_rstd = pair("x_stats", [P, T * 6]), pair("x_mv", [P, T * 2]), pair("x_rstd", [P, T])
        x_ve, y_ve, x_nm, x_shift = (pair(n, [P, T]) for n in ("x_ve", "y_ve", "x_nm", "x_shift"))
        z, z_hi, z_lo = pair("z", [P, N]), pair("z_hi", [P, N], F16), pair("z_lo", [P, N], F16)
        m_row, k_add = pair("m_row", [P, S]), pair("k_add", [P, C * S])
        k_neg, k_neg_max, k_sum = pair("k_neg", [P, C * S]), pair("k_neg_max", [P, C]), pair("k_sum", [P, C])
        ek, ek_row = pair("ek", [P, C * S]), pair("ek_row", [P, N])
        q_max, q_sub, eq = pair("q_max", [P, T * 16]), pair("q_sub", [P, N]), pair("eq", [P, N])
        eq_t, v = pair("eq_t", [P, C * S]), pair("v", [P, N])
        vcol = pair("vcol", [P, T])
        k_rsum = pair("k_rsum", [P, C])
        att_e = [pair(f"att_e{l}_", [P, C * (P + HC[l])]) for l in range(L)]
        x_plus = pair("x_plus", [P, N])
        y_rsum, y_n = pair("y_rsum", [P, T * 16]), pair("y_n", [P, N])
        y_stats, y_mv, y_rstd = pair("y_stats", [P, T * 6]), pair("y_mv", [P, T * 2]), pair("y_rstd", [P, T])
        y_nm, y_shift, y_z = pair("y_nm", [P, T]), pair("y_shift", [P, T]), pair("y_z", [P, N])
        icol = pair("icol", [P, 2 * C])
        h, th, g = pair("h", [P, N]), pair("th", [P, N]), pair("g", [P, N])
        g_hi, g_lo = pair("g_hi", [P, N], F16), pair("g_lo", [P, N], F16)

        ps_zk = bank("ps_zk")
        ps_qv = [bank(f"ps_qv{t}") for t in range(T)]
        ps_eo = bank("ps_eo")
        ps_qy = bank("ps_qy")
        ps_att = bank("ps_att")
        ps_y = [bank(f"ps_y{t}") for t in range(T)]

        const_in, cond_in, col_in, mask_in = map(sem, ("const_in", "cond_in", "col_in", "mask_in"))
        w_in_s = [sem(f"w_in{l}") for l in range(L)]
        rows_in = [sem(f"rows_in{l}") for l in range(L)]
        w_late_in = [sem(f"w_late_in{l}") for l in range(L)]
        x_in = [sem(f"x_in{i}") for i in range(4)]
        m_row_in = [sem(f"m_row_in{i}") for i in range(2)]
        mask_rows_made, mask_rows_out = sem("mask_rows_made"), sem("mask_rows_out")
        ln_b_ready, lnw_ready, w_hi_made, w_ready = map(sem, ("ln_b_ready", "lnw_ready", "w_hi_made", "w_ready"))
        wo_hi_made, wo_ready = map(sem, ("wo_hi_made", "wo_ready"))
        rows_done, rows_made, rows_hi_made = map(sem, ("rows_done", "rows_made", "rows_hi_made"))
        rows_ready, ck_done, ck_made, ck_ready = map(sem, ("rows_ready", "ck_done", "ck_made", "ck_ready"))
        film_done, film_made, film_mixed, item_col_ready = map(
            sem, ("film_done", "film_made", "film_mixed", "item_col_ready"))
        cond_tanh, cond_silu, vmask_made = map(sem, ("cond_tanh", "cond_silu", "vmask_made"))
        neg_half_made, sel_cleared, sel_made, ind_made, block_mask_made = map(
            sem, ("neg_half_made", "sel_cleared", "sel_made", "ind_made", "block_mask_made"))
        x_bn, x_stats_ready, x_powered, x_shift_ready, z_ready = map(
            sem, ("x_bn", "x_stats_ready", "x_powered", "x_shift_ready", "z_ready"))
        zt_done, z_hi_ready, z_lo_ready = map(sem, ("zt_done", "z_hi_ready", "z_lo_ready"))
        k_done, k_add_ready, k_neg_ready, ek_ready = map(sem, ("k_done", "k_add_ready", "k_neg_ready", "ek_ready"))
        qv_done = [sem(f"qv{t}_done") for t in range(T)]
        q_max_ready, q_sub_ready, v_ready, eq_ready = map(sem, ("q_max_ready", "q_sub_ready", "v_ready", "eq_ready"))
        eqt_done, ekr_done, ek_row_ready, eq_t_ready = map(sem, ("eqt_done", "ekr_done", "ek_row_ready", "eq_t_ready"))
        k_rsum_ready, ek_scaled, att_done, att_e_ready = map(
            sem, ("k_rsum_ready", "ek_scaled", "att_done", "att_e_ready"))
        y_done, y_rsum_ready, y_n_ready, y_bn, y_stats_ready = map(
            sem, ("y_done", "y_rsum_ready", "y_n_ready", "y_bn", "y_stats_ready"))
        y_powered, y_shift_ready, y_z_ready, yzt_done = map(
            sem, ("y_powered", "y_shift_ready", "y_z_ready", "yzt_done"))
        vcol_ready, icol_ready, h_ready, th_ready, g_ready, g_hi_ready, g_lo_ready = map(
            sem, ("vcol_ready", "icol_ready", "h_ready", "th_ready", "g_ready", "g_hi_ready", "g_lo_ready"))
        x_plus_ready, o_done, x_new, out_out = map(sem, ("x_plus_ready", "o_done", "x_new", "out_out"))

        block = ctx.enter_context(nc.Block())

        def wait_apart(engine, item, *waits):
            if not item.static:
                for _, value in waits:
                    engine.compute_val(value)
                engine.wait_ge(waits[0][0], 1)
            for semaphore, value in waits:
                engine.wait_ge(semaphore, value)

        def steps(engine, run, finish=None):
            for front in range(0, 6):
                run(Step(0, front))
            with engine.Fori(6, B - 1, 2) as r:
                for u in range(2):
                    run(Step(r, u, 0))
            for front in range(B, B + 6):
                run(Step(0, front))
            with engine.Fori(B + 6, LAST - 1, 2) as r:
                for u in range(2):
                    run(Step(r, u, 1))
            if finish:
                finish(*(at(Step(0, LAST), back) for back in range(1, 5)))
            else:
                for front in range(LAST, LAST + 4):
                    run(Step(0, front))

        def at(step, back):
            return Item(step, back, B, L)

        def part(tile, i, width=D):
            return tile[:, i * width:(i + 1) * width]

        @block.sync
        def _(sp):
            def load(tile, source, sem):
                sp.dma_start(tile, source).then_inc(sem, 16)

            def load_chunked(tile, source, chunks, sem):
                load(tile[:, :].rearrange("p (c n) -> p c n", c=chunks), source.rearrange("(c p) n -> p c n", p=P), sem)

            def load_sequences(first, n, sem):
                load(x_all[:, first * N:(first + n) * N].rearrange("p (a t f) -> p a t f", a=n, t=T),
                     x_dram[:, first:first + n], sem)

            load(col[:, :], columns, col_in)
            load_chunked(w_raw[0], w_in[0], C, w_in_s[0])
            load(m0r[:, :], mask0_row, mask_in)
            load(m1r[:, :], mask1_row, mask_in)
            load(row_b[0][:, :], rows[0].partition_broadcast(P), rows_in[0])
            sp.wait_ge(mask_rows_made, L)
            for l in range(L):
                sp.dma_start(mask_dram[l], m_add[l][:, :]).then_inc(mask_rows_out, 16)
            sp.wait_ge(mask_rows_out, 16 * L)

            def step(s):
                m, done = at(s, 0), at(s, 4)
                if m.exists:
                    j, p = m.index, m.parity
                    if not m.first_two:
                        sp.wait_ge(k_add_ready, j - 1)
                    if m.static:
                        row = mask_dram[m.layer, m.sequence]
                    else:
                        row = mask_dram[m.layer, bass.ds(m.sequence, 1), :].rearrange("a n -> (a n)")
                    sp.dma_start(m_row[p][:, :], row.partition_broadcast(P)).then_inc(m_row_in[p], 16)
                if s.static and s.front == 0:
                    load_sequences(2, 4, x_in[2])
                if s.static and s.front == 1:
                    load_chunked(wo_raw[0], w_out[0], C, w_late_in[0])
                    load_chunked(wemb[0], w_emb[0], EC, w_late_in[0])
                if s.static and s.front == 2:
                    load_chunked(w_raw[1], w_in[1], C, w_in_s[1])
                    load(row_b[1][:, :], rows[1].partition_broadcast(P), rows_in[1])
                if s.static and s.front == 3:
                    load_sequences(6, B - 6, x_in[3])
                    load_chunked(wo_raw[1], w_out[1], C, w_late_in[1])
                    load_chunked(wemb[1], w_emb[1], EC, w_late_in[1])
                if done.exists and done.layer == 1:
                    sp.wait_ge(x_new, done.index + 1)
                    sp.dma_start(out_dram[:, bass.ds(done.sequence, 1)],
                                 x_all[:, bass.ds(done.sequence * N, N)].rearrange("p (a t f) -> p a t f", a=1, t=T))\
                      .then_inc(out_out, 16)

            steps(sp, step)
            sp.wait_ge(out_out, 16 * B)

        @block.scalar
        def _(act):
            act.dma_start(x_all[:, 0:N].rearrange("p (t f) -> p t f", t=T), x_dram[:, 0]).then_inc(x_in[0], 16)
            act.dma_start(ident[:, :], identity).then_inc(const_in, 16)
            act.dma_start(head_ind[:, :], indicators).then_inc(const_in, 16)
            act.dma_start(x_all[:, N:2 * N].rearrange("p (t f) -> p t f", t=T), x_dram[:, 1]).then_inc(x_in[1], 16)
            act.dma_start(cond[:, :], cond_t).then_inc(cond_in, 16)
            act.dma_start(m0c[:, :], mask0_col).then_inc(cond_in, 16)
            act.dma_start(m1c[:, :], mask1_col).then_inc(cond_in, 16)

            act.wait_ge(neg_half_made, 1)
            nc.scalar.activation(act_first[:, :], neg_half[:, :], ACT.Exp)

            def cond_half_tanh():
                act.wait_ge(cond_in, 48)
                nc.scalar.activation(cond_t2[:, :], cond[:, :], ACT.Tanh, scale=0.5).then_inc(cond_tanh, 1)

            def weights_high(l):
                W = 3 * D
                act.wait_ge(lnw_ready, l + 1)
                act.wait_ge(w_in_s[l], 16)
                for c in range(C):
                    nc.scalar.activation(part(w_hi[l], c, W), part(w_raw[l], c, W), ACT.Copy,
                                         scale=lnw[l][:, c:c + 1]).then_inc(w_hi_made, 1)

            def row_biases_high(l):
                act.wait_ge(rows_made, l + 1)
                act.wait_ge(sel_made, 1)
                nc.scalar.activation(bias_hi_lo[l][0:64, :], bias_row[:, :], ACT.Copy, scale=W_SCALE)\
                  .then_inc(rows_hi_made, 1)

            def out_weights_high(l):
                act.wait_ge(w_late_in[l], 32)
                nc.scalar.activation(wo_hi[l][:, :], wo_raw[l][:, :], ACT.Copy, scale=W_SCALE).then_inc(wo_hi_made, 1)

            def z_high(a):
                j, p = a.index, a.parity
                act.wait_ge(zt_done, j + 1)
                if not a.first_two:
                    act.wait_ge(qv_done[T - 1], j - 1)
                nc.scalar.activation(z_hi[p][:, :], ps_zk[:, :], ACT.Copy, scale=Z_SCALE).then_inc(z_hi_ready, 1)

            def exp_q_turned(a):
                j, p = a.index, a.parity
                act.wait_ge(eqt_done, j + 1)
                if not a.first_two:
                    act.wait_ge(y_done, j - 1)
                nc.scalar.activation(eq_t[p][:, :], ps_qy[:, :], ACT.Copy).then_inc(eq_t_ready, 1)

            def exp_k_turned(a):
                j, p = a.index, a.parity
                act.wait_ge(ekr_done, j + 1)
                nc.scalar.activation(ek_row[p][:, :], ps_eo[:, :], ACT.Copy).then_inc(ek_row_ready, 1)

            def exp_k(a):
                j, p = a.index, a.parity
                act.wait_ge(k_neg_ready, j + 1)
                if not a.first_two:
                    act.wait_ge(ekr_done, j - 1)
                    act.wait_ge(k_rsum_ready, j - 1)
                for c in range(C):
                    last = nc.scalar.activation(part(ek[p], c), part(k_neg[p], c), ACT.Exp, scale=-1.0,
                                                bias=k_neg_max[p][:, c:c + 1], accum_out=k_sum[p][:, c:c + 1])
                last.then_inc(ek_ready, 1)

            def exp_q(a):
                j, p = a.index, a.parity
                act.wait_ge(q_sub_ready, T * j + T)
                if not a.first_two:
                    act.wait_ge(eqt_done, j - 1)
                nc.scalar.activation(eq[p][:, :], q_sub[p][:, :], ACT.Exp, scale=1.0 / QKV_SCALE).then_inc(eq_ready, 1)

            def condition(a):
                j, p = a.index, a.parity
                act.wait_ge(yzt_done, j + 1)
                act.wait_ge(icol_ready, j + 1)
                if not a.first_two:
                    act.wait_ge(g_ready, j - 1)
                for c in range(C):
                    last = nc.scalar.activation(part(h[p], c), part(ps_qy, c), ACT.Identity,
                                                scale=icol[p][:, 2 * c:2 * c + 1], bias=icol[p][:, 2 * c + 1:2 * c + 2])
                last.then_inc(h_ready, 1)

            def half_tanh(a):
                j, p = a.index, a.parity
                act.wait_ge(h_ready, j + 1)
                nc.scalar.activation(th[p][:, :], h[p][:, :], ACT.Tanh, scale=0.5).then_inc(th_ready, 1)

            def g_high(a):
                j, p = a.index, a.parity
                act.wait_ge(g_ready, j + 1)
                if not a.first_two:
                    act.wait_ge(o_done, j - 1)
                nc.scalar.activation(g_hi[p][:, :], g[p][:, :], ACT.Copy, scale=G_SCALE).then_inc(g_hi_ready, 1)

            def scale_exp_k(a):
                j, p = a.index, a.parity
                act.wait_ge(k_rsum_ready, j + 1)
                for c in range(C):
                    last = nc.scalar.activation(part(ek[p], c), part(ek[p], c), ACT.Copy, scale=k_rsum[p][:, c:c + 1])
                last.then_inc(ek_scaled, 1)

            def normalise(a):
                j, p = a.index, a.parity
                act.wait_ge(x_shift_ready, j + 1)
                if not a.first_two:
                    act.wait_ge(zt_done, j - 1)
                for t in range(T):
                    last = nc.scalar.activation(part(z[p], t), x_all[:, bass.ds(a.sequence * N + t * D, D)], ACT.Identity,
                                                scale=x_rstd[p][:, t:t + 1], bias=x_shift[p][:, t:t + 1])
                last.then_inc(z_ready, 1)

            def v_masked(a, t):
                j, p = a.index, a.parity
                act.wait_ge(q_sub_ready, T * j + t + 1)
                if t == 0:
                    act.wait_ge(vcol_ready, j + 1)
                    if not a.first_two:
                        act.wait_ge(att_done, j - 1)
                nc.scalar.activation(part(v[p], t), ps_qv[t][:, D:2 * D], ACT.Copy, scale=vcol[p][:, t:t + 1])\
                  .then_inc(v_ready, 1)

            def step(s):
                f, tz, pr, aa, o = (at(s, back) for back in range(5))
                if aa.exists:
                    exp_q_turned(aa)
                    exp_k_turned(aa)
                if tz.exists:
                    z_high(tz)
                if o.exists:
                    condition(o)
                    half_tanh(o)
                    g_high(o)
                if pr.exists:
                    exp_k(pr)
                if f.exists:
                    normalise(f)
                if pr.exists:
                    v_masked(pr, 0)
                if pr.exists and pr.layer == 1:
                    scale_exp_k(pr)
                if pr.exists:
                    exp_q(pr)
                    v_masked(pr, 1)
                if s.static and s.front == 0:
                    weights_high(0)
                    cond_half_tanh()
                if s.static and s.front == 1:
                    row_biases_high(0)
                if s.static and s.front == 2:
                    out_weights_high(0)
                if s.static and s.front == 3:
                    weights_high(1)
                    row_biases_high(1)
                if s.static and s.front == B:
                    out_weights_high(1)

            def finish(i1, i2, i3, i4):
                exp_k_turned(i3)
                exp_k(i2)
                z_high(i1)
                exp_q_turned(i3)
                v_masked(i2, 0)
                condition(i4)
                half_tanh(i4)
                exp_q(i2)
                g_high(i4)
                exp_q_turned(i2)
                v_masked(i2, 1)
                scale_exp_k(i2)
                exp_k(i1)
                condition(i3)
                half_tanh(i3)
                exp_k_turned(i2)
                g_high(i3)
                v_masked(i1, 0)
                scale_exp_k(i1)
                exp_q(i1)
                v_masked(i1, 1)
                exp_k_turned(i1)
                exp_q_turned(i1)
                condition(i2)
                half_tanh(i2)
                g_high(i2)
                condition(i1)
                half_tanh(i1)
                g_high(i1)

            steps(act, step, finish)

        @block.gpsimd
        def _(pool):
            pool.wait_ge(neg_half_made, 1)

            def indicators_in_place():
                pool.wait_ge(const_in, 32)
                first = 0
                for l in range(L):
                    for p in range(2):
                        for c in range(C):
                            base = c * (P + HC[l]) + P
                            last = pool.tensor_copy(att_e[l][p][:, base:base + HC[l]], head_ind[:, first:first + HC[l]])
                    first += HC[l]
                last.then_inc(ind_made, 1)

            def scale_and_shift(a, mv, ve, nm, rstd, shift, powered, done):
                j, p = a.index, a.parity
                pool.tensor_scalar(ve[p][:, :], mv[p][:, 1:2 * T:2], EPS, 1.0, ALU.add, ALU.mult)
                pool.tensor_scalar(nm[p][:, :], mv[p][:, 0:2 * T:2], -1.0, 0.0, ALU.mult, ALU.add).then_inc(powered, 1)
                pool.wait_ge(powered, 2 * j + 1)
                pool.tensor_tensor(rstd[p][:, :], ve[p][:, :], neg_half[:, :], ALU.pow).then_inc(powered, 1)
                pool.wait_ge(powered, 2 * j + 2)
                pool.tensor_tensor(shift[p][:, :], nm[p][:, :], rstd[p][:, :], ALU.mult).then_inc(done, 1)

            def x_scale(a):
                j, p = a.index, a.parity
                free = [] if a.first_two else [(z_ready, j - 1)]
                wait_apart(pool, a, (x_stats_ready, j + 1), *free)
                scale_and_shift(a, x_mv, x_ve, x_nm, x_rstd, x_shift, x_powered, x_shift_ready)

            def k_addend(a):
                j, p = a.index, a.parity
                if a.starts_layer:
                    pool.wait_ge(ck_ready, a.layer + 1)
                free = [] if a.first_two else [(k_neg_ready, j - 1)]
                wait_apart(pool, a, (m_row_in[p], 8 * (j - p) + 16), *free)
                for c in range(C):
                    last = pool.tensor_scalar(part(k_add[p], c), m_row[p][:, :], ck[a.layer][:, c:c + 1], 1.0,
                                              ALU.add, ALU.mult)
                last.then_inc(k_add_ready, 1)

            def v_columns(a):
                j, p = a.index, a.parity
                if a.starts_layer and a.layer == 0:
                    pool.wait_ge(vmask_made, 1)
                if not a.first_two:
                    pool.wait_ge(v_ready, T * (j - 1))
                first = a.sequence * 6 + 2 * C
                pool.tensor_copy(vcol[p][:, :], item_col[a.layer][:, bass.ds(first, T)]).then_inc(vcol_ready, 1)

            def ab_columns(a):
                j, p = a.index, a.parity
                if a.starts_layer:
                    pool.wait_ge(item_col_ready, a.layer + 1)
                if not a.first_two:
                    pool.wait_ge(h_ready, j - 1)
                pool.tensor_copy(icol[p][:, :], item_col[a.layer][:, bass.ds(a.sequence * 6, 2 * C)])\
                    .then_inc(icol_ready, 1)

            def y_normalise(a):
                j, p = a.index, a.parity
                free = [] if a.first_two else [(yzt_done, j - 1)]
                wait_apart(pool, a, (y_stats_ready, j + 1), *free)
                scale_and_shift(a, y_mv, y_ve, y_nm, y_rstd, y_shift, y_powered, y_shift_ready)
                wait_apart(pool, a, (y_shift_ready, j + 1))
                for t in range(T):
                    last = pool.tensor_scalar(part(y_z[p], t), part(y_n[p], t), y_rstd[p][:, t:t + 1],
                                              y_shift[p][:, t:t + 1], ALU.mult, ALU.add)
                last.then_inc(y_z_ready, 1)

            def add_out_bias(a):
                j, p = a.index, a.parity
                if a.starts_layer:
                    pool.wait_ge(rows_in[a.layer], 16)
                pool.wait_ge(x_stats_ready, j + 1)
                if not a.first_two:
                    pool.wait_ge(x_new, j - 1)
                pool.tensor_tensor(x_plus[p][:, :].rearrange("p (t f) -> p t f", t=T),
                                   x_all[:, bass.ds(a.sequence * N, N)].rearrange("p (t f) -> p t f", t=T),
                                   row_b[a.layer][:, bo:bo + D].unsqueeze(1).to_broadcast([P, T, D]), ALU.add)\
                    .then_inc(x_plus_ready, 1)

            def step(s):
                f, tz, o = at(s, 0), at(s, 1), at(s, 4)
                if o.exists:
                    add_out_bias(o)
                    ab_columns(o)
                    y_normalise(o)
                if f.exists:
                    x_scale(f)
                    k_addend(f)
                if tz.exists:
                    v_columns(tz)
                if s.static and s.front == 1:
                    indicators_in_place()

            def finish(i1, i2, i3, i4):
                ab_columns(i4)
                add_out_bias(i4)
                y_normalise(i4)
                y_normalise(i3)
                ab_columns(i3)
                add_out_bias(i3)
                ab_columns(i2)
                ab_columns(i1)
                v_columns(i1)
                add_out_bias(i2)
                y_normalise(i2)
                y_normalise(i1)
                add_out_bias(i1)

            steps(pool, step, finish)

        @block.vector
        def _(dve):
            vec = nc.vector

            def constants():
                vec.memset(neg_half[:, :], -0.5).then_inc(neg_half_made, 1)
                vec.memset(sel_q[:, :], 0.0).then_inc(sel_cleared, 1)
                for l in range(L):
                    vec.memset(bias_hi_lo[l][:, :], 0.0)
                dve.wait_ge(sel_cleared, 1)
                for r in (0, 32):
                    last = vec.memset(sel_q[r:r + 1, :], Z_SCALE)
                last.then_inc(sel_made, 1)

            def mask_rows():
                dve.wait_ge(mask_in, 32)
                vec.tensor_scalar(m_add[0][:, :], m0r[:, :], -1.0, MASK0 * QKV_SCALE, ALU.add, ALU.mult)\
                   .then_inc(mask_rows_made, 1)
                vec.tensor_scalar(m_add[1][:, :], m1r[:, :], 1.0, -MASK1, ALU.is_equal, ALU.mult)\
                   .then_inc(mask_rows_made, 1)

            def block_masks():
                dve.wait_ge(const_in, 32)
                first = 0
                for l in range(L):
                    last = vec.tensor_copy(block_mask[l][:, :].rearrange("p (h d) -> p h d", d=DH[l]),
                                           head_ind[:, first:first + HC[l]].unsqueeze(2).to_broadcast([P, HC[l], DH[l]]))
                    first += HC[l]
                last.then_inc(block_mask_made, 1)

            def value_masks():
                dve.wait_ge(cond_in, 48)
                for t in range(T):
                    it = [item_col[l][:, :].rearrange("p (b k) -> p k b", k=6)[:, 2 * C + t, :] for l in range(L)]
                    vec.tensor_scalar(it[0], m0c[:, t * B:(t + 1) * B], 1.0 / QKV_SCALE, None, ALU.mult)
                    last = vec.tensor_scalar(it[1], m1c[:, t * B:(t + 1) * B], 1.0, 1.0 / QKV_SCALE,
                                             ALU.not_equal, ALU.mult)
                last.then_inc(vmask_made, 1)

            def ln_bias(l):
                dve.wait_ge(col_in, 16)
                for c in range(C):
                    b = col[:, COLUMNS * l + 2 + c:COLUMNS * l + 3 + c]
                    last = vec.tensor_copy(ln_b[l][:, c * P:(c + 1) * P], b.to_broadcast([P, P]))
                last.then_inc(ln_b_ready, 1)

            def weight_scale(l):
                vec.tensor_scalar(lnw[l][:, :], col[:, COLUMNS * l:COLUMNS * l + C], W_SCALE, None, ALU.mult).then_inc(lnw_ready, 1)

            def layer_weights(l):
                W = 3 * D
                for c in range(C):
                    dve.wait_ge(w_hi_made, C * l + c + 1)
                    last = vec.scalar_tensor_tensor(part(w_lo[l], c, W), part(w_raw[l], c, W), lnw[l][:, c:c + 1],
                                                    part(w_hi[l], c, W), ALU.mult, ALU.subtract)
                last.then_inc(w_ready, 1)

            def out_weights(l):
                dve.wait_ge(wo_hi_made, l + 1)
                vec.scalar_tensor_tensor(wo_lo[l][:, :], wo_raw[l][:, :], W_SCALE, wo_hi[l][:, :],
                                         ALU.mult, ALU.subtract).then_inc(wo_ready, 1)

            def k_bias(l, bank):
                dve.wait_ge(ck_done, l + 1)
                vec.tensor_tensor(ck[l][:, :], bank[:, 0:C], col[:, COLUMNS * l + 4:COLUMNS * l + 6], ALU.add)\
                   .then_inc(ck_made, 1)
                dve.wait_ge(ck_made, l + 1)
                vec.tensor_scalar(ck[l][:, :], ck[l][:, :], QKV_SCALE, None, ALU.mult).then_inc(ck_ready, 1)

            def row_biases(l, bank):
                dve.wait_ge(rows_done, l + 1)
                dve.wait_ge(rows_in[l], 16)
                if l:
                    dve.wait_ge(rows_ready, l)
                vec.tensor_tensor(bias_row[:, :], bank[0:64, :], row_b[l][0:64, 0:2 * D], ALU.add)\
                   .then_inc(rows_made, 1)

            def row_biases_low(l):
                dve.wait_ge(rows_hi_made, l + 1)
                vec.scalar_tensor_tensor(bias_hi_lo[l][32:64, :], bias_row[32:64, :], W_SCALE,
                                         bias_hi_lo[l][32:64, :], ALU.mult, ALU.subtract).then_inc(rows_ready, 1)

            def silu_cond():
                dve.wait_ge(cond_tanh, 1)
                vec.scalar_tensor_tensor(cond_s[:, :], cond_t2[:, :], 1.0, cond[:, :], ALU.add, ALU.mult)\
                   .then_inc(cond_silu, 1)

            def film_columns(l, bank, first):
                base = COLUMNS * l
                dve.wait_ge(film_done, 2 * C * (l + 1))
                if l:
                    dve.wait_ge(item_col_ready, l)
                for e in range(2 * C):
                    last = vec.tensor_scalar(film[:, e * B:(e + 1) * B], bank[:, first + e * B:first + (e + 1) * B], 0.5,
                                             col[:, base + 6 + e:base + 7 + e], ALU.mult, ALU.add)
                last.then_inc(film_made, 1)
                dve.wait_ge(film_made, l + 1)
                it = item_col[l][:, :].rearrange("p (b k) -> p k b", k=6)
                for c in range(C):
                    l2w, l2b = col[:, base + 10 + c:base + 11 + c], col[:, base + 12 + c:base + 13 + c]
                    vec.tensor_scalar(it[:, 2 * c, :], film[:, c * B:(c + 1) * B], 1.0, l2w, ALU.add, ALU.mult)
                    last = vec.tensor_scalar(it[:, 2 * c + 1, :], film[:, c * B:(c + 1) * B], 1.0, l2b, ALU.add, ALU.mult)
                last.then_inc(film_mixed, 1)
                dve.wait_ge(film_mixed, l + 1)
                for c in range(C):
                    last = vec.tensor_tensor(it[:, 2 * c + 1, :], it[:, 2 * c + 1, :],
                                             film[:, (C + c) * B:(C + c + 1) * B], ALU.add)
                last.then_inc(item_col_ready, 1)

            def x_statistics(a):
                j, p = a.index, a.parity
                if a.static and j in (0, 1, 2):
                    dve.wait_ge(x_in[j], 16)
                if a.layer == 1:
                    dve.wait_ge(x_new, j - B + 1)
                for t in range(T):
                    last = vec.bn_stats(x_stats[p][:, 6 * t:6 * t + 6], x_all[:, bass.ds(a.sequence * N + t * D, D)])
                last.then_inc(x_bn, 1)

            def x_aggregate(a):
                j, p = a.index, a.parity
                free = [] if a.first_two else [(x_shift_ready, j - 1)]
                wait_apart(dve, a, (x_bn, j + 1), *free)
                for t in range(T):
                    last = vec.bn_aggr(x_mv[p][:, 2 * t:2 * t + 2], x_stats[p][:, 6 * t:6 * t + 6])
                last.then_inc(x_stats_ready, 1)

            def z_low(a):
                j, p = a.index, a.parity
                dve.wait_ge(z_hi_ready, j + 1)
                vec.scalar_tensor_tensor(z_lo[p][:, :], ps_zk[:, :], Z_SCALE, z_hi[p][:, :], ALU.mult, ALU.subtract)\
                   .then_inc(z_lo_ready, 1)

            def k_shift(a):
                j, p = a.index, a.parity
                free = [] if a.first_two else [(ek_ready, j - 1)]
                wait_apart(dve, a, (k_done, j + 1), (k_add_ready, j + 1), *free)
                for c in range(C):
                    last = vec.tensor_tensor_reduce(out=part(k_neg[p], c), in0=part(ps_zk, c), in1=part(k_add[p], c),
                                                    scale=-1.0 / QKV_SCALE, scalar=BIG, op0=ALU.add, op1=ALU.min,
                                                    accum_out=k_neg_max[p][:, c:c + 1])
                last.then_inc(k_neg_ready, 1)

            def q_maximum(a, t):
                j, p, l = a.index, a.parity, a.layer
                dve.wait_ge(qv_done[t], j + 1)
                q = ps_qv[t][:, 0:D].rearrange("p (h d) -> p h d", d=DH[l])
                vec.tensor_reduce(q_max[p][:, t * 16:t * 16 + HEADS[l]], q, AX_X, ALU.max).then_inc(q_max_ready, 1)

            def q_shift(a, t):
                j, p, l = a.index, a.parity, a.layer
                dve.wait_ge(q_max_ready, T * j + t + 1)
                if t == 0 and not a.first_two:
                    dve.wait_ge(eq_ready, j - 1)
                q = ps_qv[t][:, 0:D].rearrange("p (h d) -> p h d", d=DH[l])
                q_m = q_max[p][:, t * 16:t * 16 + HEADS[l]]
                vec.tensor_tensor(part(q_sub[p], t).rearrange("p (h d) -> p h d", d=DH[l]), q,
                                  q_m.unsqueeze(2).to_broadcast([P, HEADS[l], DH[l]]), ALU.subtract)\
                   .then_inc(q_sub_ready, 1)

            def k_sums(a):
                j, p = a.index, a.parity
                dve.wait_ge(ek_ready, j + 1)
                vec.reciprocal(k_rsum[p][:, :], k_sum[p][:, :]).then_inc(k_rsum_ready, 1)

            def att_scale(a):
                j, p, l = a.index, a.parity, a.layer
                dve.wait_ge(att_done, j + 1)
                if l == 0:
                    dve.wait_ge(k_rsum_ready, j + 1)
                if not a.first_two:
                    dve.wait_ge(y_done, j - 1)
                if l == 0:
                    for c in range(C):
                        base = c * (P + HC[l])
                        last = vec.scalar_tensor_tensor(att_e[l][p][:, base:base + P], part(ps_att, c, P),
                                                        k_rsum[p][:, c:c + 1], block_mask[l][:, :], ALU.mult, ALU.mult)
                else:
                    last = vec.tensor_tensor(att_e[l][p][:, :].rearrange("p (c n) -> p c n", c=C)[:, :, 0:P],
                                             ps_att[:, 0:C * P].rearrange("p (c n) -> p c n", c=C),
                                             block_mask[l][:, :].unsqueeze(1).to_broadcast([P, C, P]), ALU.mult)
                last.then_inc(att_e_ready, 1)

            def y_views(a):
                W = P + HC[a.layer]
                y = [ps_y[t][:, 0:C * W].rearrange("p (c n) -> p c n", c=C) for t in range(T)]
                r = [y_rsum[a.parity][:, t * 16:t * 16 + HEADS[a.layer]].rearrange("p (c n) -> p c n", c=C)
                     for t in range(T)]
                return [v[:, :, 0:P] for v in y], [v[:, :, P:W] for v in y], r

            def y_sums(a):
                dve.wait_ge(y_done, a.index + 1)
                _, sums, r = y_views(a)
                for t in range(T):
                    last = vec.reciprocal(r[t], sums[t])
                last.then_inc(y_rsum_ready, 1)

            def y_divide(a):
                j, p, l = a.index, a.parity, a.layer
                y, _, r = y_views(a)
                dve.wait_ge(y_rsum_ready, j + 1)
                if not a.first_two:
                    dve.wait_ge(y_z_ready, j - 1)
                for t in range(T):
                    last = vec.tensor_tensor(part(y_n[p], t).rearrange("p (c h d) -> p c h d", c=C, d=DH[l]),
                                             y[t].rearrange("p c (h d) -> p c h d", d=DH[l]),
                                             r[t].unsqueeze(3).to_broadcast([P, C, HC[l], DH[l]]), ALU.mult)
                last.then_inc(y_n_ready, 1)

            def y_statistics(a):
                j, p = a.index, a.parity
                dve.wait_ge(y_n_ready, j + 1)
                for t in range(T):
                    last = vec.bn_stats(y_stats[p][:, 6 * t:6 * t + 6], part(y_n[p], t))
                last.then_inc(y_bn, 1)

            def y_aggregate(a):
                j, p = a.index, a.parity
                wait_apart(dve, a, (y_bn, j + 1))
                for t in range(T):
                    last = vec.bn_aggr(y_mv[p][:, 2 * t:2 * t + 2], y_stats[p][:, 6 * t:6 * t + 6])
                last.then_inc(y_stats_ready, 1)

            def gate(a):
                j, p = a.index, a.parity
                dve.wait_ge(th_ready, j + 1)
                vec.scalar_tensor_tensor(g[p][:, :], th[p][:, :], 1.0, h[p][:, :], ALU.add, ALU.mult).then_inc(g_ready, 1)

            def g_low(a):
                j, p = a.index, a.parity
                dve.wait_ge(g_hi_ready, j + 1)
                vec.scalar_tensor_tensor(g_lo[p][:, :], g[p][:, :], G_SCALE, g_hi[p][:, :], ALU.mult, ALU.subtract)\
                   .then_inc(g_lo_ready, 1)

            def residual(a):
                j = a.index
                dve.wait_ge(o_done, j + 1)
                dve.wait_ge(x_plus_ready, j + 1)
                vec.scalar_tensor_tensor(x_all[:, bass.ds(a.sequence * N, N)], ps_eo[:, :], 1.0 / OUT_SCALE,
                                         x_plus[a.parity][:, :], ALU.mult, ALU.add).then_inc(x_new, 1)

            constants()
            for l in range(L):
                ln_bias(l)
                weight_scale(l)

            def step(s):
                f, tz, pr, aa, o = (at(s, back) for back in range(5))
                if f.exists:
                    x_statistics(f)
                if tz.exists:
                    z_low(tz)
                if f.exists:
                    x_aggregate(f)
                if pr.exists:
                    q_maximum(pr, 0)
                if s.static and s.front == 0:
                    mask_rows()
                    block_masks()
                    k_bias(0, ps_y[0])
                if s.static and s.front == 1:
                    layer_weights(0)
                if aa.exists:
                    att_scale(aa)
                if o.exists:
                    gate(o)
                if pr.exists:
                    q_maximum(pr, 1)
                    q_shift(pr, 0)
                if o.exists:
                    g_low(o)
                if aa.exists:
                    y_sums(aa)
                    y_divide(aa)
                if pr.exists:
                    k_sums(pr)
                if aa.exists:
                    y_statistics(aa)
                    y_aggregate(aa)
                if s.static and s.front == 1:
                    value_masks()
                    row_biases(0, ps_att)
                    row_biases_low(0)
                if pr.exists:
                    q_shift(pr, 1)
                if o.exists:
                    residual(o)
                if tz.exists:
                    k_shift(tz)
                if s.static and s.front == 1:
                    silu_cond()
                if s.static and s.front == 2:
                    film_columns(0, ps_y[0], 0)
                if s.static and s.front == 3:
                    out_weights(0)
                    row_biases(1, ps_att)
                if s.static and s.front == 4:
                    row_biases_low(1)
                    k_bias(1, ps_att)
                    layer_weights(1)
                if s.static and s.front == 5:
                    dve.wait_ge(x_in[3], 16)
                if s.static and s.front == B + 1:
                    out_weights(1)
                if s.static and s.front == B + 2:
                    film_columns(1, ps_att, C * P)

            def finish(i1, i2, i3, i4):
                q_maximum(i2, 0)
                att_scale(i3)
                q_shift(i2, 0)
                q_maximum(i2, 1)
                z_low(i1)
                q_shift(i2, 1)
                y_sums(i3)
                y_divide(i3)
                gate(i4)
                y_statistics(i3)
                y_aggregate(i3)
                k_sums(i2)
                q_maximum(i1, 0)
                g_low(i4)
                k_shift(i1)
                residual(i4)
                gate(i3)
                g_low(i3)
                k_sums(i1)
                q_shift(i1, 0)
                att_scale(i2)
                q_maximum(i1, 1)
                q_shift(i1, 1)
                residual(i3)
                y_sums(i2)
                y_divide(i2)
                y_statistics(i2)
                y_aggregate(i2)
                att_scale(i1)
                y_sums(i1)
                y_divide(i1)
                y_statistics(i1)
                y_aggregate(i1)
                gate(i2)
                g_low(i2)
                gate(i1)
                residual(i2)
                g_low(i1)
                residual(i1)

            steps(dve, step, finish)

        @block.tensor
        def _(pe):
            mm, turn = nc.tensor.matmul, nc.tensor.transpose
            W = 3 * D

            def row_bias_products(l, bank):
                if l:
                    pe.wait_ge(w_in_s[l], 16)
                    pe.wait_ge(att_e_ready, 1)
                for c in range(C):
                    last = mm(bank[:, :], ln_b[l][:, c * P:(c + 1) * P], w_raw[l][:, c * W + D:(c + 1) * W],
                              start=(c == 0), stop=(c == C - 1))
                last.then_inc(rows_done, 1)

            def k_bias_products(l, bank):
                if l:
                    pe.wait_ge(att_e_ready, 2)
                else:
                    pe.wait_ge(w_in_s[l], 16)
                    pe.wait_ge(ln_b_ready, L)
                for d in range(C):
                    for c in range(C):
                        last = mm(bank[:, d:d + 1], w_raw[l][:, c * W + d * P:c * W + (d + 1) * P],
                                  ln_b[l][:, c * P:c * P + 1], start=(c == 0), stop=(c == C - 1))
                last.then_inc(ck_done, 1)

            def film_products(l, bank, first, parts):
                if parts[0] == 0:
                    pe.wait_ge(w_late_in[l], 32)
                    pe.wait_ge(cond_silu, 1)
                    pe.wait_ge(ck_made, l + 1)
                for e in parts:
                    for c in range(EC):
                        last = mm(bank[:, first + e * B:first + (e + 1) * B],
                                  wemb[l][:, c * 2 * D + e * P:c * 2 * D + (e + 1) * P],
                                  cond_s[:, c * B:(c + 1) * B], start=(c == 0), stop=(c == EC - 1))
                    last.then_inc(film_done, 1)

            def turn_z(a):
                j, p = a.index, a.parity
                pe.wait_ge(z_ready, j + 1)
                if not (a.static and a.index == 0):
                    pe.wait_ge(k_neg_ready, j)
                for c in range(C):
                    for t in range(T):
                        last = turn(ps_zk[:, c * S + t * P:c * S + (t + 1) * P],
                                    z[p][:, t * D + c * P:t * D + (c + 1) * P], ident[:, :])
                last.then_inc(zt_done, 1)

            def project_k(a):
                j, p, l = a.index, a.parity, a.layer
                pe.wait_ge(z_lo_ready, j + 1)
                if a.starts_layer:
                    pe.wait_ge(w_ready, l + 1)
                for d in range(C):
                    n = 0
                    for c in range(C):
                        for w, zz in ((w_hi, z_hi), (w_hi, z_lo), (w_lo, z_hi)):
                            last = mm(part(ps_zk, d), w[l][:, c * W + d * P:c * W + (d + 1) * P], part(zz[p], c),
                                      start=(n == 0), stop=(n == 3 * C - 1))
                            n += 1
                last.then_inc(k_done, 1)

            def project_qv(a, t):
                j, p, l = a.index, a.parity, a.layer
                if a.starts_layer and t == 0:
                    pe.wait_ge(rows_ready, l + 1)
                    pe.wait_ge(sel_made, 1)
                if not (a.static and a.index == 0):
                    pe.wait_ge(v_ready, T * (j - 1) + t + 1)
                n = 0
                for c in range(C):
                    for zz, w in ((z_hi, w_hi), (z_hi, w_lo), (z_lo, w_hi)):
                        last = mm(ps_qv[t][:, :], zz[p][:, c * S + t * P:c * S + (t + 1) * P], w[l][:, c * W + D:(c + 1) * W],
                           start=(n == 0), stop=(n == 3 * C - 1))
                        if n == 0:
                            mm(ps_qv[t][:, :], sel_q[:, :], bias_hi_lo[l][:, :], start=False, stop=False)
                        n += 1
                last.then_inc(qv_done[t], 1)

            def turn_exp_q(a):
                j, p = a.index, a.parity
                pe.wait_ge(eq_ready, j + 1)
                if not a.first_two:
                    pe.wait_ge(h_ready, j - 1)
                for c in range(C):
                    for t in range(T):
                        last = turn(ps_qy[:, c * S + t * P:c * S + (t + 1) * P],
                                    eq[p][:, t * D + c * P:t * D + (c + 1) * P], ident[:, :])
                last.then_inc(eqt_done, 1)

            def turn_exp_k(a):
                j, p = a.index, a.parity
                if a.layer == 0:
                    pe.wait_ge(ek_ready, j + 1)
                else:
                    pe.wait_ge(ek_scaled, j - B + 1)
                if not a.first_two:
                    pe.wait_ge(x_new, j - 1)
                for t in range(T):
                    for c in range(C):
                        last = turn(ps_eo[:, t * D + c * P:t * D + (c + 1) * P],
                                    ek[p][:, c * S + t * P:c * S + (t + 1) * P], ident[:, :])
                last.then_inc(ekr_done, 1)

            def attend(a):
                j, p, l = a.index, a.parity, a.layer
                pe.wait_ge(ek_row_ready, j + 1)
                pe.wait_ge(v_ready, T * j + T)
                if a.static and a.index in (0, 1):
                    pe.wait_ge(rows_made, a.index + 1)
                if a.static and a.index == 2:
                    pe.wait_ge(ck_made, 2)
                if a.static and a.index == B:
                    pe.wait_ge(film_made, 2)
                if not (a.static and a.index == 0):
                    pe.wait_ge(att_e_ready, j)
                left, right = (ek_row, v) if l == 0 else (v, ek_row)
                for c in range(C):
                    for t in range(T):
                        tile = slice(t * D + c * P, t * D + (c + 1) * P)
                        last = mm(part(ps_att, c, P), left[p][:, tile], right[p][:, tile],
                                  start=(t == 0), stop=(t == T - 1))
                last.then_inc(att_done, 1)

            def attention_out(a):
                j, p, l = a.index, a.parity, a.layer
                E = P + HC[l]
                pe.wait_ge(eq_t_ready, j + 1)
                pe.wait_ge(att_e_ready, j + 1)
                if a.static and a.index == 0:
                    pe.wait_ge(ind_made, 1)
                    pe.wait_ge(film_made, 1)
                else:
                    pe.wait_ge(y_n_ready, j)
                for t in range(T):
                    for c in range(C):
                        last = mm(part(ps_y[t], c, E), eq_t[p][:, c * S + t * P:c * S + (t + 1) * P],
                                  part(att_e[l][p], c, E), start=True, stop=True)
                last.then_inc(y_done, 1)

            def turn_y(a):
                j, p = a.index, a.parity
                pe.wait_ge(y_z_ready, j + 1)
                if a.next_exists:
                    pe.wait_ge(eq_t_ready, j + 2)
                else:
                    pe.wait_ge(h_ready, j)
                for c in range(C):
                    for t in range(T):
                        last = turn(ps_qy[:, c * S + t * P:c * S + (t + 1) * P],
                                    y_z[p][:, t * D + c * P:t * D + (c + 1) * P], ident[:, :])
                last.then_inc(yzt_done, 1)

            def project_out(a):
                j, p, l = a.index, a.parity, a.layer
                pe.wait_ge(g_lo_ready, j + 1)
                if a.starts_layer:
                    pe.wait_ge(wo_ready, l + 1)
                if a.next_exists:
                    pe.wait_ge(ek_row_ready, j + 2)
                else:
                    pe.wait_ge(x_new, j)
                for t in range(T):
                    n = 0
                    for c in range(C):
                        for gg, w in ((g_hi, wo_hi), (g_hi, wo_lo), (g_lo, wo_hi)):
                            last = mm(part(ps_eo, t), gg[p][:, c * S + t * P:c * S + (t + 1) * P], part(w[l], c),
                                      start=(n == 0), stop=(n == 3 * C - 1))
                            n += 1
                last.then_inc(o_done, 1)

            k_bias_products(0, ps_y[0])
            pe.wait_ge(const_in, 32)

            def step(s):
                tz, pr, aa, o = (at(s, back) for back in range(1, 5))
                if pr.exists:
                    project_qv(pr, 0)
                if aa.exists:
                    turn_exp_q(aa)
                    turn_exp_k(aa)
                if tz.exists:
                    turn_z(tz)
                if o.exists:
                    turn_y(o)
                if s.static and s.front == 1:
                    row_bias_products(0, ps_att)
                if aa.exists:
                    attend(aa)
                if pr.exists:
                    project_qv(pr, 1)
                if aa.exists:
                    attention_out(aa)
                if tz.exists:
                    project_k(tz)
                if s.static and B <= s.front <= B + 2:
                    film_products(1, ps_att, C * P, ((0, 1), (2,), (3,))[s.front - B])
                if o.exists:
                    project_out(o)
                if s.static and s.front == 2:
                    film_products(0, ps_y[0], 0, range(2 * C))
                if s.static and s.front == 3:
                    row_bias_products(1, ps_att)
                if s.static and s.front == 4:
                    k_bias_products(1, ps_att)

            def finish(i1, i2, i3, i4):
                project_qv(i2, 0)
                turn_exp_k(i3)
                turn_exp_q(i3)
                turn_z(i1)
                attend(i3)
                project_qv(i2, 1)
                turn_y(i4)
                attention_out(i3)
                project_k(i1)
                project_qv(i1, 0)
                turn_exp_q(i2)
                project_out(i4)
                turn_y(i3)
                turn_exp_k(i2)
                project_qv(i1, 1)
                attend(i2)
                project_out(i3)
                attention_out(i2)
                turn_exp_k(i1)
                turn_exp_q(i1)
                attend(i1)
                attention_out(i1)
                turn_y(i2)
                turn_y(i1)
                project_out(i2)
                project_out(i1)

            steps(pe, step, finish)


def kernel(**inputs):
    import numpy as np
    import concourse.bacc as bacc
    from concourse.bass_utils import run_bass_kernel_spmd as run

    f = {n: np.asarray(a) for n, a in inputs.items()}
    P, B, S = 128, f["x"].shape[0], f["x"].shape[1]
    names = [dict(lw="L0_cond_ln_w", lb="L0_cond_ln_b", q="L0_cond_Wq", bq="L0_cond_bq", k="L0_cond_Wk", bk="L0_cond_bk",
                  v="L0_cond_Wv", bv="L0_cond_bv", e="L0_cond_W_emb", be="L0_cond_b_emb", l2w="L0_cond_ln2_w",
                  l2b="L0_cond_ln2_b", o="L0_cond_W_out", bo="L0_cond_b_out"),
             dict(lw="L1_cond_norm_scale", lb="L1_cond_norm_bias", q="L1_cond_Wq", bq="L1_cond_bq", k="L1_cond_Wk",
                  bk="L1_cond_bk", v="L1_cond_Wv", bv="L1_cond_bv", e="L1_cond_film_emb_W", be="L1_cond_film_emb_b",
                  l2w="L1_cond_film_norm_scale", l2b="L1_cond_film_norm_bias", o="L1_cond_film_out_W",
                  bo="L1_cond_film_out_b")]

    def column(a):
        return a.reshape(-1, P).T

    def head_indicators():
        return np.concatenate([np.arange(P)[:, None] // d == np.arange(P // d)[None, :] for d in (32, 16)], 1)

    arrays = {
        "x": f["x"],
        "cond_t": f["cond_2048"].T.reshape(-1, P, B).transpose(1, 0, 2).reshape(P, -1),
        "mask0_row": f["mask_BxSx1_fk1"].reshape(B, S),
        "mask1_row": f["mask_BxS_ik0"],
        "mask0_col": f["mask_BxSx1_fk1"].reshape(B, S // P, P).transpose(2, 1, 0).reshape(P, -1),
        "mask1_col": f["mask_BxS_ik0"].reshape(B, S // P, P).transpose(2, 1, 0).reshape(P, -1),
        "identity": np.eye(P, dtype=np.float32),
        "indicators": head_indicators().astype(np.float32),
        "columns": np.concatenate([np.concatenate([column(f[n[i]]) for i in ("lw", "lb", "bk", "be", "l2w", "l2b")], 1)
                                   for n in names], 1),
        "rows": np.stack([np.concatenate([f[n[i]] for i in ("bq", "bv", "bo")]) for n in names]),
        "w_in": np.stack([np.concatenate([f[n[i]] for i in ("k", "q", "v")], 1) for n in names]),
        "w_emb": np.stack([f[n["e"]] for n in names]),
        "w_out": np.stack([f[n["o"]] for n in names]),
    }
    arrays = {n: np.ascontiguousarray(a) for n, a in arrays.items()}
    nc = bacc.Bacc("TRN2", target_bir_lowering=False, num_devices=1)
    aps = {n: nc.dram_tensor(f"in_{n}", a.shape, mybir.dt.from_np(a.dtype), kind="ExternalInput").ap()
           for n, a in arrays.items()}
    out = nc.dram_tensor("out_0", f["x"].shape, F32, kind="ExternalOutput").ap()
    two_layers(nc, out=out, **aps)
    r = run(nc, [{f"in_{n}": a for n, a in arrays.items()}], core_ids=[0])
    return r.results[0]["out_0"]
```
